# Optimizing a Trainium2 kernel written in Bass

```python
import numpy as np
import jax
import jax.numpy as jnp

def _softmax(x, axis=-1):
    return jax.nn.softmax(x, axis=axis)

def _gelu(x):
    return jax.nn.gelu(x, approximate=True)

def _silu(x):
    return jax.nn.silu(x)

def _sigmoid(x):
    return jax.nn.sigmoid(x)

def _layernorm(x, axis=-1, eps=1e-05):
    m = jnp.mean(x, axis=axis, keepdims=True)
    v = jnp.var(x, axis=axis, keepdims=True)
    return (x - m) / jnp.sqrt(v + eps)

def _scatter_add(tgt, idx, src, axis=0):
    return tgt.at[idx].add(src)

def _segment_sum(src, seg, n):
    return jax.ops.segment_sum(src, seg, n)
kernel_name = 'mk_lm_tower_d1_tok_ids1024_r4_026ec1'

def setup_inputs(seed: int=0):
    np.random.seed(seed)
    _w = jnp.asarray

    def _rec_inputs():
        import jax
        import jax.numpy as jnp
        _rk = jax.random.key(seed)
        x = jax.random.randint(jax.random.fold_in(_rk, 1), (2, 1024), 0, 12564, jnp.int32)
        return x
    x = _rec_inputs()

    def _L0_tok_setup():
        import jax, jax.numpy as jnp
        import numpy as np
        VOCAB, DIM, N_DOM, EXP = (50257, 256, 8, 32)
        B, S = (4, 1024)
        key = jax.random.key(seed)
        k1, k2, k3, k4, k5, k6 = jax.random.split(key, 6)
        token_ids = jax.random.randint(k1, (B, S), 0, VOCAB, dtype=jnp.int32)
        dom = jax.random.randint(k2, (VOCAB,), 0, N_DOM, dtype=jnp.int32)
        routed = jax.random.uniform(k3, (VOCAB,)) < 0.2
        domain_map = jnp.where(routed, dom, jnp.int32(-1))
        emb_table = jax.random.normal(k4, (VOCAB, DIM), dtype=jnp.float32) * 0.02
        lim_e = 0.1 * np.sqrt(6.0 / (DIM + EXP))
        lim_p = 0.1 * np.sqrt(6.0 / (EXP + DIM))
        W_exp = jax.random.uniform(k5, (N_DOM, EXP, DIM), minval=-lim_e, maxval=lim_e, dtype=jnp.float32)
        W_proj = jax.random.uniform(k6, (N_DOM, DIM, EXP), minval=-lim_p, maxval=lim_p, dtype=jnp.float32)
        return {'token_ids': token_ids, 'domain_map': domain_map, 'emb_table': emb_table, 'W_exp': W_exp, 'W_proj': W_proj}
    _L0_tok_all = _L0_tok_setup()
    _L0_tok_in = {k: v for k, v in _L0_tok_all.items() if k in ('domain_map', 'emb_table', 'W_exp', 'W_proj')}
    del _L0_tok_all

    def _L0_attn_setup():
        import jax, jax.numpy as jnp
        import numpy as np
        import math
        B, L, D, H = (4, 1024, 256, 16)
        d = D // H

        def _stp_forward(x, Wqkv_w, Wqkv_b, out_w, out_b, W_static, Lambda_raw, Gamma):
            b, l, dm = x.shape
            scale = 1.0 / math.sqrt(d)
            qkv = x @ Wqkv_w.T + Wqkv_b
            qkv = qkv.reshape(b, l, 3, H, d)
            qkv = jnp.transpose(qkv, (2, 0, 3, 1, 4))
            q, k, v = (qkv[0], qkv[1], qkv[2])
            k = k * scale
            retention = 1.0 - jax.nn.sigmoid(Lambda_raw)
            qs = jnp.moveaxis(q, 2, 0)
            ks_ = jnp.moveaxis(k, 2, 0)
            vs = jnp.moveaxis(v, 2, 0)

            def step(state, qkv_t):
                q_t, k_t, v_t = qkv_t
                hebbian = jnp.einsum('bhi,bhj->bhij', v_t, k_t)
                state = retention[None] * state + Gamma[None] * hebbian
                y_t = jnp.einsum('bhij,bhj->bhi', W_static[None] + state, q_t)
                return (state, y_t)
            state0 = jnp.zeros((b, H, d, d), dtype=x.dtype)
            _, ys = jax.lax.scan(step, state0, (qs, ks_, vs))
            y = jnp.transpose(ys, (1, 0, 2, 3)).reshape(b, l, dm)
            return y @ out_w.T + out_b
        key = jax.random.key(seed)
        ks = jax.random.split(key, 8)
        s = 0.02
        x = jax.random.normal(ks[0], (B, L, D), dtype=jnp.float32)
        Wqkv_w = jax.random.normal(ks[1], (3 * D, D), dtype=jnp.float32) * s
        Wqkv_b = jnp.zeros((3 * D,), dtype=jnp.float32)
        out_w = jax.random.normal(ks[2], (D, D), dtype=jnp.float32) * s
        out_b = jnp.zeros((D,), dtype=jnp.float32)
        W_static = jax.random.normal(ks[3], (H, d, d), dtype=jnp.float32) * s
        Lambda_raw = jax.random.uniform(ks[4], (H, d, d), dtype=jnp.float32, minval=-3.0, maxval=3.0)
        g = 0.5 / math.sqrt(d)
        Gamma = jax.random.uniform(ks[5], (H, d, d), dtype=jnp.float32, minval=-g, maxval=g)
        return {'x': x, 'Wqkv_w': Wqkv_w, 'Wqkv_b': Wqkv_b, 'out_w': out_w, 'out_b': out_b, 'W_static': W_static, 'Lambda_raw': Lambda_raw, 'Gamma': Gamma}
    _L0_attn_all = _L0_attn_setup()
    _L0_attn_in = {k: v for k, v in _L0_attn_all.items() if k in ('Wqkv_w', 'Wqkv_b', 'out_w', 'out_b', 'W_static', 'Lambda_raw', 'Gamma')}
    del _L0_attn_all

    def _L0_ffn_setup():
        import jax, jax.numpy as jnp
        import numpy as np
        QMAX = 127.0
        EPS = 1e-08

        def _quantize_per_token(x):
            amax = jnp.clip(jnp.max(jnp.abs(x), axis=-1, keepdims=True), EPS, None)
            scale = amax / QMAX
            x_q = jnp.clip(jnp.round(x / scale), -128, 127)
            return (x_q, scale)

        def _quantize_per_channel(w):
            amax = jnp.clip(jnp.max(jnp.abs(w), axis=-1, keepdims=True), EPS, None)
            scale = amax / QMAX
            w_q = jnp.clip(jnp.round(w / scale), -128, 127)
            return (w_q, scale)
        key = jax.random.key(seed)
        k1, k2, k3 = jax.random.split(key, 3)
        B, S, DIN, DOUT = (8, 1024, 256, 256)
        x = jax.random.normal(k1, (B, S, DIN), dtype=jnp.float32)
        weight = jax.random.normal(k2, (DOUT, DIN), dtype=jnp.float32) * 0.02
        bias = jax.random.normal(k3, (DOUT,), dtype=jnp.float32)
        return {'x': x, 'weight': weight, 'bias': bias}
    _L0_ffn_all = _L0_ffn_setup()
    _L0_ffn_in = {k: v for k, v in _L0_ffn_all.items() if k in ('weight', 'bias')}
    del _L0_ffn_all
    return {'x': x, 'L0_tok_domain_map': _L0_tok_in['domain_map'], 'L0_tok_emb_table': _L0_tok_in['emb_table'], 'L0_tok_W_exp': _L0_tok_in['W_exp'], 'L0_tok_W_proj': _L0_tok_in['W_proj'], 'L0_attn_Wqkv_w': _L0_attn_in['Wqkv_w'], 'L0_attn_Wqkv_b': _L0_attn_in['Wqkv_b'], 'L0_attn_out_w': _L0_attn_in['out_w'], 'L0_attn_out_b': _L0_attn_in['out_b'], 'L0_attn_W_static': _L0_attn_in['W_static'], 'L0_attn_Lambda_raw': _L0_attn_in['Lambda_raw'], 'L0_attn_Gamma': _L0_attn_in['Gamma'], 'L0_ffn_weight': _L0_ffn_in['weight'], 'L0_ffn_bias': _L0_ffn_in['bias']}

def reference(x, L0_tok_domain_map, L0_tok_emb_table, L0_tok_W_exp, L0_tok_W_proj, L0_attn_Wqkv_w, L0_attn_Wqkv_b, L0_attn_out_w, L0_attn_out_b, L0_attn_W_static, L0_attn_Lambda_raw, L0_attn_Gamma, L0_ffn_weight, L0_ffn_bias):
    import jax
    import jax.numpy as jnp

    def _L0_tok_ref(token_ids, domain_map, emb_table, W_exp, W_proj):
        import jax, jax.numpy as jnp
        import numpy as np
        VOCAB, DIM, N_DOM, EXP = (50257, 256, 8, 32)
        B, S = (4, 1024)
        base = emb_table[token_ids]
        dom = domain_map[token_ids]
        out = base
        n_domains = W_exp.shape[0]
        for d in range(n_domains):
            mask = (dom == d)[..., None].astype(base.dtype)
            expanded = jnp.einsum('bsd,ed->bse', base, W_exp[d])
            corr = jnp.einsum('bse,de->bsd', expanded, W_proj[d])
            out = out + 0.1 * corr * mask
        return out

    def _L0_attn_ref(x, Wqkv_w, Wqkv_b, out_w, out_b, W_static, Lambda_raw, Gamma):
        import jax, jax.numpy as jnp
        import numpy as np
        import math
        B, L, D, H = (4, 1024, 256, 16)
        d = D // H

        def _stp_forward(x, Wqkv_w, Wqkv_b, out_w, out_b, W_static, Lambda_raw, Gamma):
            b, l, dm = x.shape
            scale = 1.0 / math.sqrt(d)
            qkv = x @ Wqkv_w.T + Wqkv_b
            qkv = qkv.reshape(b, l, 3, H, d)
            qkv = jnp.transpose(qkv, (2, 0, 3, 1, 4))
            q, k, v = (qkv[0], qkv[1], qkv[2])
            k = k * scale
            retention = 1.0 - jax.nn.sigmoid(Lambda_raw)
            qs = jnp.moveaxis(q, 2, 0)
            ks_ = jnp.moveaxis(k, 2, 0)
            vs = jnp.moveaxis(v, 2, 0)

            def step(state, qkv_t):
                q_t, k_t, v_t = qkv_t
                hebbian = jnp.einsum('bhi,bhj->bhij', v_t, k_t)
                state = retention[None] * state + Gamma[None] * hebbian
                y_t = jnp.einsum('bhij,bhj->bhi', W_static[None] + state, q_t)
                return (state, y_t)
            state0 = jnp.zeros((b, H, d, d), dtype=x.dtype)
            _, ys = jax.lax.scan(step, state0, (qs, ks_, vs))
            y = jnp.transpose(ys, (1, 0, 2, 3)).reshape(b, l, dm)
            return y @ out_w.T + out_b
        return _stp_forward(x, Wqkv_w, Wqkv_b, out_w, out_b, W_static, Lambda_raw, Gamma)

    def _L0_ffn_ref(x, weight, bias):
        import jax, jax.numpy as jnp
        import numpy as np
        QMAX = 127.0
        EPS = 1e-08

        def _quantize_per_token(x):
            amax = jnp.clip(jnp.max(jnp.abs(x), axis=-1, keepdims=True), EPS, None)
            scale = amax / QMAX
            x_q = jnp.clip(jnp.round(x / scale), -128, 127)
            return (x_q, scale)

        def _quantize_per_channel(w):
            amax = jnp.clip(jnp.max(jnp.abs(w), axis=-1, keepdims=True), EPS, None)
            scale = amax / QMAX
            w_q = jnp.clip(jnp.round(w / scale), -128, 127)
            return (w_q, scale)
        B, S, DIN = x.shape
        w_q, w_scale = _quantize_per_channel(weight.astype(jnp.float32))
        x_flat = x.reshape(-1, DIN).astype(jnp.float32)
        x_q, x_scale = _quantize_per_token(x_flat)
        out = jnp.matmul(x_q, w_q.T) * x_scale * w_scale.T
        out = out.reshape(B, S, -1) + bias
        return out.astype(x.dtype)
    h = _L0_tok_ref(x, L0_tok_domain_map, L0_tok_emb_table, L0_tok_W_exp, L0_tok_W_proj)
    h = h + _L0_attn_ref(_layernorm(h, axis=-1), L0_attn_Wqkv_w, L0_attn_Wqkv_b, L0_attn_out_w, L0_attn_out_b, L0_attn_W_static, L0_attn_Lambda_raw, L0_attn_Gamma)
    h = h + _L0_ffn_ref(_layernorm(h, axis=-1), L0_ffn_weight, L0_ffn_bias)
    return h

_drawn_inputs = setup_inputs


def setup_inputs(seed=0):
    import zlib

    import numpy as np

    out = dict(_drawn_inputs(seed))
    spreads = {'L0_attn_Wqkv_b': (0.0, 0.8), 'L0_attn_out_b': (0.0, 2.0)}
    factors = {'L0_tok_W_exp': 56.125,
     'L0_tok_W_proj': 57.013,
     'L0_attn_Lambda_raw': 8.0,
     'L0_attn_Gamma': 8.0,
     'L0_attn_W_static': 64.0,
     'L0_ffn_weight': 5.826}
    for name, (base, spread) in spreads.items():
        noise = np.random.default_rng([zlib.crc32(name.encode()), seed]).standard_normal(out[name].shape)
        drawn = base * np.exp(spread * noise) if base else spread * noise
        out[name] = jnp.asarray(drawn.astype(out[name].dtype))
    for name, factor in factors.items():
        out[name] = (out[name] * factor).astype(out[name].dtype)
    return out
```

```python
from contextlib import ExitStack

import numpy as np

import concourse.bass as bass
from concourse import mybir
from concourse.alu_op_type import AluOpType as ALU

F32 = mybir.dt.float32
BF16 = mybir.dt.bfloat16
I32 = mybir.dt.int32
ACT = mybir.ActivationFunctionType
AX = mybir.AxisListType

P = 128
BATCH, SEQ, DIM, HEADS, HD = 2, 1024, 256, 16, 16
TOKENS = BATCH * SEQ
NTILE = TOKENS // P
T = 512
TT = T // P
NC = TOKENS // T
KD = DIM // P
HG = HEADS * HD // P
UNITS = HG * HD
NB = 4
NA = HD // NB
PARTS = 3
NDOM, EXP = 8, 32
ROUND = 12582912.0
QMAX, QEPS, LNEPS = 127.0, 1e-8, 1e-5

LAG = 8
LEAD = 4
NVR, NVG, NU, NZ = 2, 4, 4, 8

FRONT, BACK, OWN, SETUP = 1, -1, 0, 9
PE_PLAN = [(0, OWN, "q1"), (5, BACK, "attn"), (7, FRONT, "base_t"), (8.5, FRONT, "expand"), (10, BACK, "xq_t"),
           (12, BACK, "ffn"), (14, FRONT, "masked_t"), (15.5, FRONT, "corr"), (18, FRONT, "xhat_t"),
           (20, FRONT, "v"), (22, FRONT, "k"), (24, FRONT, "q0")]
ACT_PLAN = [(1, OWN, "q1"), (4, BACK, "y1"), (6.4, BACK, "sqrt2"), (7.3, BACK, "xhat2"), (8, FRONT, "base_t"),
            (9, BACK, "quant"), (11, BACK, "xq_t"), (15, FRONT, "masked_t"), (16.4, FRONT, "sqrt1"),
            (17.3, FRONT, "xhat"), (19, FRONT, "xhat_t"), (20, OWN, "y0"), (21, FRONT, "v"), (22.5, FRONT, "k"),
            (23.5, FRONT, "v_mid"), (25, FRONT, "q0")]
DVE_PLAN = [(6, BACK, "attn"), (7, BACK, "rstd2"), (8, BACK, "amax"), (9.5, FRONT, "mask"), (13, BACK, "out"),
            (16, FRONT, "corr"), (17, FRONT, "rstd1")]
POOL_PLAN = [(9, BACK, "bias"), (22, FRONT, "v_res"), (24, FRONT, "v_lo")]
SETUP_AT = {"tensor": (5, "w_t"), "scalar": [(4, "w_round"), (6, "w_hi"), (9, "w_mid")],
            "vector": [(3, "w_amax"), (5, "w_deq"), (7, "w_res"), (10, "w_lo")]}


def calendar(plan, setup, lead):
    at = {}
    for phase in range(-1, NC + 1):
        for tau, kind, name in plan:
            c = phase + kind
            if 0 <= c < NC:
                at.setdefault(phase * UNITS + int(tau) + lead, []).append((tau + phase * UNITS, name, c))
    for tau, name in setup:
        at.setdefault(int(tau) + lead, []).append((tau, name, 0))
    return {slot: [(name, c) for _, name, c in sorted(todo)] for slot, todo in at.items()}


def tower_kernel(nc, ids, domain_map, table, w_exp, w_proj, w_q, w_k, w_v, b_q, b_k, b_v, w_o, b_o,
                 static, lam, gam, w_f, b_f, dom_of_col, ident, first_row, sel_v, sel_y, out):
    pe_at = calendar(PE_PLAN, [SETUP_AT["tensor"]], LEAD)
    act_at = calendar(ACT_PLAN, SETUP_AT["scalar"], LEAD)
    dve_at = calendar(DVE_PLAN, SETUP_AT["vector"], 0)
    pool_at = calendar(POOL_PLAN, [], 0)
    SLOTS = range(-UNITS, (NC + 1) * UNITS)
    uses = [key for slot in SLOTS for key in pe_at.get(slot, [])]
    use = {key: n for n, key in enumerate(uses)}

    def unit(g):
        c, n = divmod(g, UNITS)
        hg, m = divmod(n, HD)
        return c, n, hg, m % NA, m // NA

    with ExitStack() as ctx:
        def sb(name, shape, dt=F32):
            return ctx.enter_context(nc.sbuf_tensor(name, shape, dt))

        def ps(name, shape, dt=F32):
            return ctx.enter_context(nc.psum_tensor(name, shape, dt))

        def sem(name):
            return ctx.enter_context(nc.semaphore(name))

        ids_sb = sb("ids_sb", [P, NTILE], I32)
        wexp = sb("wexp", [P, KD, NDOM * EXP])
        wproj = sb("wproj", [P, KD, DIM])
        wq = sb("wq", [P, KD, DIM])
        wk = sb("wk", [P, KD, DIM])
        wv = sb("wv", [P, KD, DIM])
        wo = sb("wo", [P, HG, DIM])
        wf = sb("wf", [P, KD, DIM])
        wf_parts = sb("wf_parts", [P, PARTS, KD, DIM], BF16)
        bq = sb("bq", [P, HG])
        bk = sb("bk", [P, HG])
        bk4 = sb("bk4", [P, HG])
        bv = sb("bv", [P, HG])
        bo = sb("bo", [P, DIM])
        bf = sb("bf", [P, DIM])
        wst = sb("wst", [P, UNITS])
        lam_sb = sb("lam_sb", [P, UNITS])
        gam_sb = sb("gam_sb", [P, UNITS])
        domcol = sb("domcol", [P, NDOM * EXP])
        idf = sb("idf", [P, P])
        idb = sb("idb", [P, P], BF16)
        row0 = sb("row0", [P, P])
        selv32 = sb("selv32", [PARTS * 32, NB, P])
        selv = sb("selv", [PARTS * 32, NB, P], BF16)
        sely = sb("sely", [P, NB, 32])
        rnd = sb("rnd", [P, 1])
        rnd_neg = sb("rnd_neg", [P, 1])
        dom_i = sb("dom_i", [P, NTILE], I32)
        dom_f = sb("dom_f", [P, NTILE])
        tok = sb("tok", [P, NTILE, DIM])
        act_t = sb("act_t", [P, KD, T])
        tmp_f = sb("tmp_f", [P, TT, DIM])
        tmp_b = sb("tmp_b", [P, TT, DIM])
        xq = sb("xq", [P, TT, DIM], BF16)
        xq_t = sb("xq_t", [P, KD, T], BF16)
        kk = sb("kk", [P, 2, HG, T])
        vv = sb("vv", [P, HG, T])
        v_part = [sb(f"v_part{p}", [P, HG, T], BF16) for p in range(PARTS)]
        v_rows = sb("v_rows", [PARTS * 32, 2, HG, NA, T], BF16)
        y_t = sb("y_t", [P, HG, T])
        vg = sb("vg", [P, NVG, T])
        uu = sb("uu", [P, NU, T])
        state = sb("state", [P, UNITS, T])
        zz = sb("zz", [P, NZ, T])
        bn = sb("bn", [P, 2, TT, 6])
        mv = sb("mv", [P, 2, TT, 2])
        ve = sb("ve", [P, 2, TT])
        sd = sb("sd", [P, 2, TT])
        nr = sb("nr", [P, 2, 4, TT])
        rstd = sb("rstd", [P, 2, TT])
        nmr = sb("nmr", [P, 2, TT])
        am = sb("am", [P, TT])
        xs = sb("xs", [P, TT])
        xinv = sb("xinv", [P, TT])
        wam = sb("wam", [P, KD])
        ws = sb("ws", [P, KD])
        winv = sb("winv", [P, KD])

        vr_ps = ps("vr_ps", [P, NVR, T])
        q_ps = ps("q_ps", [P, HG, T])
        y_ps = ps("y_ps", [P, T])
        scr = ps("scr", [P, 2, T])
        r_ps = ps("r_ps", [P, T])
        scr_tok = scr[:, :, :].rearrange("p a (b d) -> p (a b) d", d=DIM)
        scr_bf = scr[:, 0, :].bitcast(BF16).rearrange("p (k t) -> p k t", k=KD)

        s_ids = sem("s_ids")
        s_w_tok, s_w_tok2, s_w_qkv, s_w_unit, s_w_back = (sem(n) for n in ("s_w_tok", "s_w_tok2", "s_w_qkv", "s_w_unit", "s_w_back"))
        s_base = [sem(f"s_base{c}") for c in range(NC)]
        s_const = sem("s_const")
        s_cast = sem("s_cast")
        s_sig = sem("s_sig")
        s_ret = sem("s_ret")
        s_full = sem("s_full")
        s_free = sem("s_free")
        s_var = [sem("s_var1"), sem("s_var2")]
        s_sqrt = [sem("s_sqrt1"), sem("s_sqrt2")]
        s_rstd = [sem("s_rstd1"), sem("s_rstd2")]
        s_xhat = [sem("s_xhat1"), sem("s_xhat2")]
        s_vhi = sem("s_vhi")
        s_vres = sem("s_vres")
        s_vmid = sem("s_vmid")
        s_vlo = sem("s_vlo")
        s_vrows = sem("s_vrows")
        s_amax = sem("s_amax")
        s_xq = sem("s_xq")
        s_h2b = sem("s_h2b")
        s_stored = sem("s_stored")
        s_vr = sem("s_vr")
        s_vg = sem("s_vg")
        s_u = sem("s_u")
        s_scan = sem("s_scan")
        s_z = sem("s_z")
        s_y = sem("s_y")
        s_yt = sem("s_yt")
        s_wq = sem("s_wq")
        s_dve = sem("s_dve")

        block = ctx.enter_context(nc.Block())

        @block.sync
        def _(sp):
            sp.dma_start(ids_sb[:], ids).then_inc(s_ids, 16)
            for dst, src in ((idf, ident), (wexp, w_exp), (domcol, dom_of_col)):
                sp.dma_start(dst[:], src).then_inc(s_w_tok, 16)
            sp.dma_start(wproj[:], w_proj).then_inc(s_w_tok2, 16)
            for dst, src in ((wv, w_v), (bv, b_v), (wk, w_k), (bk, b_k), (wq, w_q), (bq, b_q)):
                sp.dma_start(dst[:], src).then_inc(s_w_qkv, 16)
            for dst, src in ((lam_sb, lam), (gam_sb, gam), (wst, static), (selv32, sel_v), (sely, sel_y)):
                sp.dma_start(dst[:], src).then_inc(s_w_unit, 16)
            for dst, src in ((wf, w_f), (wo, w_o), (bo, b_o), (row0, first_row), (bf, b_f)):
                sp.dma_start(dst[:], src).then_inc(s_w_back, 16)
            out_v = out.rearrange("b (c t p) d -> (b c) p t d", c=SEQ // T, p=P)

            def move_v(c):
                if c >= 2:
                    sp.wait_ge(s_vr, UNITS * (c - 1))
                for p, ready in enumerate((s_vhi, s_vmid, s_vlo)):
                    sp.wait_ge(ready, c + 1)
                    for a in range(NA):
                        sp.dma_start(v_rows[32 * p:32 * p + 32, c % 2, :, a, :],
                                     v_part[p][32 * a:32 * a + 32, :, :]).then_inc(s_vrows, 16)

            def store(c):
                sp.wait_ge(s_free, use["ffn", c] + 1)
                sp.dma_start(out_v[c], tok[:, TT * c:TT * c + TT, :]).then_inc(s_stored, 16)

            move_v(0)
            for c in range(1, NC):
                if c >= 2:
                    store(c - 2)
                move_v(c)
            store(NC - 2)
            store(NC - 1)
            sp.wait_ge(s_stored, 16 * NC)

        @block.gpsimd
        def _(pool):
            pool.wait_ge(s_ids, 16)
            for c in range(NC):
                for t in range(TT * c, TT * c + TT):
                    ix = bass.IndirectOffsetOnAxis(ap=ids_sb[:, t:t + 1], axis=0)
                    pool.indirect_dma_start(tok[:, t, :], None, table, ix).then_inc(s_base[c], 16)
                for t in range(TT * c, TT * c + TT):
                    ix = bass.IndirectOffsetOnAxis(ap=ids_sb[:, t:t + 1], axis=0)
                    pool.indirect_dma_start(dom_i[:, t:t + 1], None, domain_map, ix).then_inc(s_base[c], 16)

            def v_res(c):
                pool.wait_ge(s_vhi, c + 1)
                pool.tensor_tensor(vv[:], vv[:], v_part[0][:], ALU.subtract).then_inc(s_vres, 1)

            def v_lo(c):
                pool.wait_ge(s_vmid, c + 1)
                if c >= 1:
                    pool.wait_ge(s_vrows, 16 * PARTS * NA * c)
                pool.tensor_tensor(v_part[2][:], vv[:], v_part[1][:], ALU.subtract).then_inc(s_vlo, 1)

            def bias(c):
                pool.wait_ge(s_xhat[1], c + 1)
                if c == 0:
                    pool.wait_ge(s_w_back, 80)
                h = tok[:, TT * c:TT * c + TT, :]
                pool.tensor_tensor(h, h, bf[:].rearrange("p (o d) -> p o d", o=1).to_broadcast([P, TT, DIM]),
                                   ALU.add).then_inc(s_h2b, 1)

            stage = {"v_res": v_res, "v_lo": v_lo, "bias": bias}
            for slot in SLOTS:
                if 0 <= slot < NC * UNITS:
                    c, n, hg, a, b = unit(slot)
                    if n == 0:
                        pool.wait_ge(s_free, use["k", c] + 1)
                    pool.wait_ge(s_vg, slot + 1)
                    if slot >= NU:
                        pool.wait_ge(s_scan, slot - NU + 1)
                    pool.tensor_tensor(uu[:, slot % NU, :], vg[:, slot % NVG, :], kk[:, c % 2, hg, :],
                                       ALU.mult).then_inc(s_u, 1)
                for name, c in pool_at.get(slot, []):
                    stage[name](c)

        @block.scalar
        def _(act):
            act.wait_ge(s_w_tok, 48)
            act.activation(idb[:], idf[:], ACT.Copy).then_inc(s_cast, 1)
            act.wait_ge(s_w_unit, 80)
            act.activation(lam_sb[:], lam_sb[:], ACT.Sigmoid).then_inc(s_sig, 1)
            act.activation(selv[:], selv32[:], ACT.Copy).then_inc(s_cast, 1)
            act.wait_ge(s_w_tok2, 16)
            act.activation(wproj[:], wproj[:], ACT.Copy, scale=0.1).then_inc(s_cast, 1)
            act.wait_ge(s_w_qkv, 96)
            act.activation(bk4[:], bk[:], ACT.Copy, scale=0.25).then_inc(s_cast, 1)
            act.wait_ge(s_cast, 4)

            def evacuate(dst, name):
                def step(c):
                    act.wait_ge(s_full, use[name, c] + 1)
                    act.activation(dst, scr[:], ACT.Copy).then_inc(s_free, 1)
                return step

            def q_half(hg):
                def step(c):
                    act.wait_ge(s_full, use[f"q{hg}", c] + 1)
                    if c >= 1:
                        act.wait_ge(s_z, UNITS * (c - 1) + HD * (hg + 1))
                    act.activation(q_ps[:, hg, :], scr[:, 0, :], ACT.Identity, bias=bq[:, hg:hg + 1])\
                       .then_inc(s_free, 1)
                return step

            def v(c):
                act.wait_ge(s_full, use["v", c] + 1)
                if c >= 1:
                    act.wait_ge(s_vlo, c)
                    act.wait_ge(s_vrows, 16 * PARTS * NA * c)
                for hg in range(HG):
                    last = act.activation(vv[:, hg, :], scr[:, hg, :], ACT.Identity, bias=bv[:, hg:hg + 1])
                last.then_inc(s_free, 1)
                act.wait_ge(s_free, use["v", c] + 1)
                act.activation(v_part[0][:], vv[:], ACT.Copy).then_inc(s_vhi, 1)

            def v_mid(c):
                act.wait_ge(s_vres, c + 1)
                act.activation(v_part[1][:], vv[:], ACT.Copy).then_inc(s_vmid, 1)

            def k(c):
                act.wait_ge(s_full, use["k", c] + 1)
                if c >= 2:
                    act.wait_ge(s_u, UNITS * (c - 1))
                for hg in range(HG):
                    last = act.activation(kk[:, c % 2, hg, :], scr[:, hg, :], ACT.Identity, bias=bk4[:, hg:hg + 1],
                                          scale=HD ** -0.5)
                last.then_inc(s_free, 1)

            def y_half(hg):
                def step(c):
                    act.wait_ge(s_y, (UNITS * c + HD * (hg + 1)) // NA)
                    if c >= 1:
                        act.wait_ge(s_full, use["attn", c - 1] + 1)
                    act.activation(y_t[:, hg, :], y_ps[:], ACT.Copy).then_inc(s_yt, 1)
                return step

            def sqrt(n):
                def step(c):
                    act.wait_ge(s_var[n], c + 1)
                    act.activation(sd[:, n, :], ve[:, n, :], ACT.Sqrt).then_inc(s_sqrt[n], 1)
                return step

            def xhat(n, dst):
                def step(c):
                    act.wait_ge(s_rstd[n], c + 1)
                    for t in range(TT):
                        last = act.activation(dst[:, t, :], tok[:, TT * c + t, :], ACT.Identity,
                                              bias=nmr[:, n, t:t + 1], scale=rstd[:, n, t:t + 1])
                    last.then_inc(s_xhat[n], 1)
                return step

            def quant(c):
                act.wait_ge(s_amax, c + 1)
                for t in range(TT):
                    last = act.activation(tmp_b[:, t, :], tmp_b[:, t, :], ACT.Identity, bias=rnd[:],
                                          scale=xinv[:, t:t + 1])
                last.then_inc(s_cast, 1)
                act.wait_ge(s_cast, 5 + c)
                act.activation(xq[:], tmp_b[:], ACT.Identity, bias=rnd_neg[:]).then_inc(s_xq, 1)

            def xq_evac(c):
                act.wait_ge(s_full, use["xq_t", c] + 1)
                act.activation(xq_t[:], scr_bf, ACT.Copy).then_inc(s_free, 1)

            def w_round(_):
                act.wait_ge(s_wq, 1)
                for k_ in range(KD):
                    last = act.activation(wf[:, k_, :], wf[:, k_, :], ACT.Identity, bias=rnd[:],
                                          scale=winv[:, k_:k_ + 1])
                last.then_inc(s_wq, 1)

            def w_hi(_):
                act.wait_ge(s_full, use["w_t", 0] + 1)
                act.activation(wf_parts[:, 0], scr_tok[:, 0:KD, :], ACT.Copy).then_inc(s_wq, 1)

            def w_mid(_):
                act.wait_ge(s_free, use["w_t", 0] + 1)
                act.activation(wf_parts[:, 1], wf[:], ACT.Copy).then_inc(s_wq, 1)

            stage = {"base_t": evacuate(act_t[:], "base_t"), "masked_t": evacuate(act_t[:], "masked_t"),
                     "xhat_t": evacuate(act_t[:], "xhat_t"), "q0": q_half(0), "q1": q_half(1), "v": v,
                     "v_mid": v_mid, "k": k, "y0": y_half(0), "y1": y_half(1), "sqrt1": sqrt(0), "sqrt2": sqrt(1),
                     "xhat": xhat(0, tmp_f), "xhat2": xhat(1, tmp_b), "quant": quant, "xq_t": xq_evac,
                     "w_round": w_round, "w_hi": w_hi, "w_mid": w_mid}
            for slot in SLOTS:
                if 0 <= slot < NC * UNITS:
                    act.wait_ge(s_vr, slot + 1)
                    if slot >= NVG:
                        act.wait_ge(s_u, slot - NVG + 1)
                    n = slot % UNITS
                    act.activation(vg[:, slot % NVG, :], vr_ps[:, slot % NVR, :], ACT.Copy,
                                   scale=gam_sb[:, n:n + 1]).then_inc(s_vg, 1)
                for name, c in act_at.get(slot, []):
                    stage[name](c)

        @block.vector
        def _(dve):
            chain = [0]

            def link(ins):
                chain[0] += 1
                ins.then_inc(s_dve, 1)
                dve.wait_ge(s_dve, chain[0])

            dve.memset(rnd[:], ROUND)
            dve.memset(rnd_neg[:], -ROUND).then_inc(s_const, 1)
            dve.wait_ge(s_sig, 1)
            dve.tensor_scalar(r_ps[:, 0:UNITS], lam_sb[:], -1.0, 1.0, ALU.mult, ALU.add).then_inc(s_ret, 1)

            def mask(c):
                ts = slice(TT * c, TT * c + TT)
                link(dve.tensor_copy(dom_f[:, ts], dom_i[:, ts]))
                dve.wait_ge(s_full, use["expand", c] + 1)
                for t in range(TT):
                    last = dve.scalar_tensor_tensor(tmp_f[:, t, :], domcol[:], dom_f[:, TT * c + t:TT * c + t + 1],
                                                    scr_tok[:, t, :], ALU.is_equal, ALU.mult)
                last.then_inc(s_free, 1)

            def residual(n, name):
                def step(c):
                    dve.wait_ge(s_full, use[name, c] + 1)
                    h = tok[:, TT * c:TT * c + TT, :]
                    dve.tensor_tensor(h, h, scr_tok, ALU.add).then_inc(s_free, 1)
                    dve.wait_ge(s_free, use[name, c] + 1)
                    for t in range(TT):
                        last = dve.bn_stats(bn[:, n, t, :], tok[:, TT * c + t, :])
                    link(last)
                    for t in range(TT):
                        last = dve.bn_aggr(mv[:, n, t, :], bn[:, n, t, :])
                    link(last)
                    dve.tensor_scalar(ve[:, n, :], mv[:, n, :, 1], LNEPS, None, ALU.add).then_inc(s_var[n], 1)
                return step

            def rsqrt(n):
                def step(c):
                    dve.wait_ge(s_sqrt[n], c + 1)
                    r0, sq, vs, fix = (nr[:, n, i, :] for i in range(4))
                    link(dve.reciprocal(r0, sd[:, n, :]))
                    link(dve.tensor_tensor(sq, r0, r0, ALU.mult))
                    link(dve.tensor_tensor(vs, sq, ve[:, n, :], ALU.mult))
                    link(dve.tensor_scalar(fix, vs, -0.5, 1.5, ALU.mult, ALU.add))
                    link(dve.tensor_tensor(rstd[:, n, :], r0, fix, ALU.mult))
                    dve.scalar_tensor_tensor(nmr[:, n, :], mv[:, n, :, 0], -1.0, rstd[:, n, :], ALU.mult,
                                             ALU.mult).then_inc(s_rstd[n], 1)
                return step

            def amax(c):
                dve.wait_ge(s_xhat[1], c + 1)
                link(dve.tensor_reduce(am[:], tmp_b[:], AX.X, ALU.max, apply_absolute_value=True))
                link(dve.tensor_scalar(xs[:], am[:], QEPS, 1.0 / QMAX, ALU.max, ALU.mult))
                dve.reciprocal(xinv[:], xs[:]).then_inc(s_amax, 1)

            def finish(c):
                dve.wait_ge(s_full, use["ffn", c] + 1)
                dve.wait_ge(s_h2b, c + 1)
                for t in range(TT):
                    h = tok[:, TT * c + t, :]
                    last = dve.scalar_tensor_tensor(h, scr_tok[:, t, :], xs[:, t:t + 1], h, ALU.mult, ALU.add)
                last.then_inc(s_free, 1)

            def w_amax(_):
                dve.wait_ge(s_w_back, 80)
                link(dve.tensor_reduce(wam[:], wf[:], AX.X, ALU.max, apply_absolute_value=True))
                link(dve.tensor_scalar(ws[:], wam[:], QEPS, 1.0 / QMAX, ALU.max, ALU.mult))
                dve.reciprocal(winv[:], ws[:]).then_inc(s_wq, 1)

            def w_deq(_):
                dve.wait_ge(s_wq, 2)
                for k_ in range(KD):
                    last = dve.tensor_scalar(wf[:, k_, :], wf[:, k_, :], -ROUND, ws[:, k_:k_ + 1], ALU.add, ALU.mult)
                last.then_inc(s_wq, 1)

            def w_res(_):
                dve.wait_ge(s_wq, 4)
                dve.tensor_tensor(wf[:], scr_tok[:, 0:KD, :], wf_parts[:, 0], ALU.subtract).then_inc(s_free, 1)

            def w_lo(_):
                dve.wait_ge(s_wq, 5)
                dve.tensor_tensor(wf_parts[:, 2], wf[:], wf_parts[:, 1], ALU.subtract).then_inc(s_wq, 1)

            def scan(g):
                c, n, hg, a, b = unit(g)
                dve.wait_ge(s_u, g + 1)
                start = 0.0 if c % (SEQ // T) == 0 else state[:, n, T - 1:T]
                dve.tensor_tensor_scan(state[:, n, :], r_ps[:, n:n + 1].to_broadcast([P, T]), uu[:, g % NU, :],
                                       start, ALU.mult, ALU.add).then_inc(s_scan, 1)

            def product(g):
                c, n, hg, a, b = unit(g)
                if n % HD == 0:
                    dve.wait_ge(s_free, use[f"q{hg}", c] + 1)
                dve.wait_ge(s_scan, g + 1)
                if g >= NZ:
                    dve.wait_ge(s_y, (g - NZ) // NA + 1)
                dve.scalar_tensor_tensor(zz[:, g % NZ, :], state[:, n, :], wst[:, n:n + 1], q_ps[:, hg, :], ALU.add,
                                         ALU.mult).then_inc(s_z, 1)

            stage = {"mask": mask, "corr": residual(0, "corr"), "rstd1": rsqrt(0), "attn": residual(1, "attn"),
                     "rstd2": rsqrt(1), "amax": amax, "out": finish, "w_amax": w_amax, "w_deq": w_deq,
                     "w_res": w_res, "w_lo": w_lo}
            dve.wait_ge(s_w_tok, 48)
            for slot in SLOTS:
                if 0 <= slot < NC * UNITS:
                    if slot == 0:
                        dve.wait_ge(s_ret, 1)
                    scan(slot)
                if 0 < slot <= NC * UNITS:
                    product(slot - 1)
                for name, c in dve_at.get(slot, []):
                    if name == "mask":
                        dve.wait_ge(s_base[c], 16 * 2 * TT)
                    stage[name](c)

        @block.tensor
        def _(pe):
            def scratch(name, c):
                if use[name, c]:
                    pe.wait_ge(s_free, use[name, c])

            def transposes(name, src, ready):
                def step(c):
                    scratch(name, c)
                    pe.wait_ge(*ready(c))
                    for t in range(TT):
                        for k_ in range(KD):
                            last = pe.transpose(scr[:, k_, P * t:P * t + P], src(c, t)[:, P * k_:P * k_ + P], idf[:])
                    last.then_inc(s_full, 1)
                return step

            def token_major(name, weight):
                def step(c):
                    scratch(name, c)
                    if name == "corr":
                        pe.wait_ge(s_cast, 3)
                    for t in range(TT):
                        for k_ in range(KD):
                            last = pe.matmul(scr_tok[:, t, :], act_t[:, k_, P * t:P * t + P], weight[:, k_, :],
                                             start=(k_ == 0), stop=(k_ == KD - 1))
                    last.then_inc(s_full, 1)
                return step

            def channel_major(name, weight, groups):
                def step(c):
                    scratch(name, c)
                    for at, hg in enumerate(groups):
                        for k_ in range(KD):
                            last = pe.matmul(scr[:, at, :], weight[:, k_, P * hg:P * hg + P], act_t[:, k_, :],
                                             start=(k_ == 0), stop=(k_ == KD - 1))
                    last.then_inc(s_full, 1)
                return step

            def attn(c):
                scratch("attn", c)
                pe.wait_ge(s_yt, HG * (c + 1))
                if c == 0:
                    pe.wait_ge(s_w_back, 80)
                for t in range(TT):
                    pe.matmul(scr_tok[:, t, :], row0[:], bo[:], start=True, stop=False)
                    for hg in range(HG):
                        last = pe.matmul(scr_tok[:, t, :], y_t[:, hg, P * t:P * t + P], wo[:, hg, :],
                                         start=False, stop=(hg == HG - 1))
                last.then_inc(s_full, 1)

            def xq_transposes(c):
                scratch("xq_t", c)
                pe.wait_ge(s_xq, c + 1)
                for t in range(TT):
                    for k_ in range(KD):
                        last = pe.transpose(scr_bf[:, k_, P * t:P * t + P], xq[:, t, P * k_:P * k_ + P], idb[:])
                last.then_inc(s_full, 1)

            def ffn(c):
                scratch("ffn", c)
                if c == 0:
                    pe.wait_ge(s_wq, 6)
                for t in range(TT):
                    for n in range(PARTS * KD):
                        p, k_ = n // KD, n % KD
                        last = pe.matmul(scr_tok[:, t, :], xq_t[:, k_, P * t:P * t + P], wf_parts[:, p, k_, :],
                                         start=(n == 0), stop=(n == PARTS * KD - 1))
                last.then_inc(s_full, 1)

            def w_t(_):
                scratch("w_t", 0)
                pe.wait_ge(s_wq, 3)
                for k_ in range(KD):
                    for o in range(KD):
                        last = pe.transpose(scr_tok[:, k_, P * o:P * o + P], wf[:, o, P * k_:P * k_ + P], idf[:])
                last.then_inc(s_full, 1)

            stage = {"base_t": transposes("base_t", lambda c, t: tok[:, TT * c + t, :], lambda c: (s_base[c], 16 * 2 * TT)),
                     "expand": token_major("expand", wexp),
                     "masked_t": transposes("masked_t", lambda c, t: tmp_f[:, t, :], lambda c: (s_free, use["expand", c] + 1)),
                     "corr": token_major("corr", wproj),
                     "xhat_t": transposes("xhat_t", lambda c, t: tmp_f[:, t, :], lambda c: (s_xhat[0], c + 1)),
                     "v": channel_major("v", wv, range(HG)), "k": channel_major("k", wk, range(HG)),
                     "q0": channel_major("q0", wq, [0]), "q1": channel_major("q1", wq, [1]),
                     "attn": attn, "xq_t": xq_transposes, "ffn": ffn, "w_t": w_t}

            def spread(g):
                c, n, hg, a, b = unit(g)
                if n == 0:
                    pe.wait_ge(s_vrows, 16 * PARTS * NA * (c + 1))
                if g >= NVR:
                    pe.wait_ge(s_vg, g - NVR + 1)
                pe.matmul(vr_ps[:, g % NVR, :], selv[:, b, :], v_rows[:, c % 2, hg, a, :], start=True, stop=True)\
                  .then_inc(s_vr, 1)

            def collect(g):
                c, n, hg, a, b = unit(g)
                if n % HD == 0 and g > 0:
                    pe.wait_ge(s_yt, g // HD)
                pe.wait_ge(s_z, g + NA)
                for a in range(NA):
                    last = pe.matmul(y_ps[32 * a:32 * a + 32, :], sely[:, b, :], zz[:, (g + a) % NZ, :],
                                     start=(b == 0), stop=(b == NB - 1))
                last.then_inc(s_y, 1)

            pe.wait_ge(s_w_tok, 48)
            for slot in SLOTS:
                if slot == 0:
                    pe.wait_ge(s_cast, 4)
                if 0 <= slot < NC * UNITS:
                    spread(slot)
                g = slot - LAG - NA + 1
                if g >= 0 and g % NA == 0 and g < NC * UNITS:
                    collect(g)
                for name, c in pe_at.get(slot, []):
                    if (name, c) == ("v", 0):
                        pe.wait_ge(s_w_qkv, 96)
                    stage[name](c)


def kernel(**inputs):
    import concourse.bacc as _bacc
    from concourse.bass_utils import run_bass_kernel_spmd as _run

    def halves(m):
        return m.reshape(KD, P, -1).transpose(1, 0, 2)

    g = {k: np.asarray(v) for k, v in inputs.items()}
    rows = np.arange(DIM).reshape(HG, P // HD, NA, NB).transpose(0, 2, 1, 3).reshape(-1)
    w_qkv, b_qkv = g["L0_attn_Wqkv_w"], g["L0_attn_Wqkv_b"]

    def per_unit(m):
        m = m.reshape(HG, P // HD, NA, NB, HD).transpose(1, 4, 0, 3, 2)
        return m.reshape(P, UNITS)

    h8 = np.arange(P) // HD
    sel_v = np.zeros((PARTS, P // HD, NB, NB, P), np.float32)
    sel_y = np.zeros((P, NB, P // HD, NB), np.float32)
    for b in range(NB):
        for h in range(P // HD):
            sel_v[:, h, b, b, h8 == h] = 1.0
            sel_y[h8 == h, b, h, b] = 1.0
    first_row = np.zeros((P, P), np.float32)
    first_row[0] = 1.0
    arrays = {
        "ids": g["x"].reshape(NTILE, P).T,
        "domain_map": g["L0_tok_domain_map"].reshape(-1, 1),
        "table": g["L0_tok_emb_table"],
        "w_exp": halves(g["L0_tok_W_exp"].reshape(NDOM * EXP, DIM).T),
        "w_proj": halves(g["L0_tok_W_proj"].transpose(0, 2, 1).reshape(NDOM * EXP, DIM)),
        "w_q": halves(w_qkv[:DIM].T),
        "w_k": halves(w_qkv[DIM:2 * DIM].T),
        "w_v": halves(w_qkv[2 * DIM:][rows].T),
        "b_q": b_qkv[:DIM].reshape(HG, P).T,
        "b_k": b_qkv[DIM:2 * DIM].reshape(HG, P).T,
        "b_v": b_qkv[2 * DIM:][rows].reshape(HG, P).T,
        "w_o": halves(g["L0_attn_out_w"].T[rows]),
        "b_o": np.broadcast_to(g["L0_attn_out_b"], (P, DIM)),
        "static": per_unit(g["L0_attn_W_static"]),
        "lam": per_unit(g["L0_attn_Lambda_raw"]),
        "gam": per_unit(g["L0_attn_Gamma"]),
        "w_f": halves(g["L0_ffn_weight"]),
        "b_f": np.broadcast_to(g["L0_ffn_bias"], (P, DIM)),
        "dom_of_col": np.broadcast_to(np.arange(NDOM * EXP, dtype=np.float32) // EXP, (P, NDOM * EXP)),
        "ident": np.eye(P, dtype=np.float32),
        "first_row": first_row,
        "sel_v": sel_v.reshape(PARTS * 32, NB, P),
        "sel_y": sel_y.reshape(P, NB, 32),
    }
    nc = _bacc.Bacc("TRN2", target_bir_lowering=False, num_devices=1)
    args = {}
    for name, a in arrays.items():
        arrays[name] = a = np.ascontiguousarray(a)
        args[name] = nc.dram_tensor(f"in_{name}", a.shape, mybir.dt.from_np(a.dtype), kind="ExternalInput").ap()
    out = nc.dram_tensor("out_h", (BATCH, SEQ, DIM), F32, kind="ExternalOutput").ap()
    tower_kernel(nc, out=out, **args)
    r = _run(nc, [{f"in_{name}": a for name, a in arrays.items()}], core_ids=[0])
    return r.results[0]["out_h"]
```

```python
from contextlib import ExitStack

import numpy as np

import concourse.bass as bass
from concourse import mybir
from concourse.alu_op_type import AluOpType as ALU

F32 = mybir.dt.float32
BF16 = mybir.dt.bfloat16
I32 = mybir.dt.int32
ACT = mybir.ActivationFunctionType
AX = mybir.AxisListType

P = 128
BATCH, SEQ, DIM, HEADS, HD = 2, 1024, 256, 16, 16
TOKENS = BATCH * SEQ
NTILE = TOKENS // P
T = 512
TT = T // P
NC = TOKENS // T
KD = DIM // P
HG = HEADS * HD // P
UNITS = HG * HD
NB = 4
NA = HD // NB
PARTS = 3
NDOM, EXP = 8, 32
ROUND = 12582912.0
QMAX, QEPS, LNEPS = 127.0, 1e-8, 1e-5

LAG = 8
LEAD = 4
NVR, NVG, NU, NZ = 2, 8, 8, 16

FRONT, BACK, OWN = 1, -1, 0
PE_PLAN = [(5.39, OWN, "q", 1), (5.56, BACK, "attn", 0), (6.06, BACK, "attn", 1), (7.95, FRONT, "base_t", 0),
           (8.45, FRONT, "base_t", 1), (9.54, FRONT, "expand", 0), (10.05, FRONT, "expand", 1),
           (11.01, BACK, "xq_t", 0), (11.42, BACK, "xq_t", 1), (12.62, BACK, "ffn", 0), (12.88, BACK, "ffn", 1),
           (13.7, FRONT, "masked_t", 0), (14.2, FRONT, "masked_t", 1), (15.04, FRONT, "corr", 0),
           (15.74, FRONT, "corr", 1), (18.15, FRONT, "xhat_t", 0), (18.65, FRONT, "xhat_t", 1),
           (20.53, FRONT, "v", 0), (21.5, FRONT, "v", 1), (21.69, FRONT, "v_less", 0), (21.81, FRONT, "v_less", 1),
           (22.15, FRONT, "v_less2", 0), (22.35, FRONT, "v_less2", 1), (25.41, FRONT, "k", 0), (27.36, FRONT, "k", 1),
           (29.24, FRONT, "q", 0)]
ACT_PLAN = [(4.17, BACK, "y", 1), (5.74, OWN, "q", 1), (6.06, BACK, "attn", 0), (6.46, BACK, "attn", 1),
            (6.75, BACK, "sqrt2", 0), (7.15, BACK, "sqrt2", 1), (8.3, BACK, "xhat2", 0), (8.45, FRONT, "base_t", 0),
            (8.7, BACK, "xhat2", 1), (9.16, FRONT, "base_t", 1), (9.82, BACK, "quant", 0), (10.22, BACK, "quant", 1),
            (11.42, BACK, "xq_t", 0), (11.92, BACK, "xq_t", 1), (14.5, FRONT, "masked_t", 0),
            (14.9, FRONT, "masked_t", 1), (15.99, FRONT, "corr", 0), (16.63, FRONT, "corr", 1),
            (17.54, FRONT, "sqrt1", 0), (17.94, FRONT, "sqrt1", 1), (18.44, FRONT, "xhat", 0),
            (18.84, FRONT, "xhat", 1), (19.15, FRONT, "xhat_t", 1), (19.39, FRONT, "xhat_t", 0), (20.06, OWN, "y", 0),
            (20.42, FRONT, "v_hi", 0), (21.04, FRONT, "v_hi", 1), (21.57, FRONT, "v_mid", 0),
            (22.07, FRONT, "v_mid", 1), (22.75, FRONT, "v_lo", 0), (23.92, FRONT, "v_lo", 1), (26.11, FRONT, "k", 0),
            (27.31, FRONT, "k", 1), (30.24, FRONT, "q", 0)]
DVE_PLAN = [(7, BACK, "stat2", 0), (7.3, BACK, "stat2", 1), (8, BACK, "rstd2", 0), (8.12, BACK, "rstd2", 1),
            (8.96, BACK, "amax", 0), (9.36, BACK, "amax", 1), (10.68, FRONT, "mask", 0), (11.18, FRONT, "mask", 1),
            (14.07, BACK, "out", 0), (14.47, BACK, "out", 1), (16.99, FRONT, "stat1", 0), (17.14, FRONT, "stat1", 1),
            (17.27, FRONT, "rstd1", 0), (17.67, FRONT, "rstd1", 1)]
POOL_PLAN = [(-32.4, FRONT, "gather", 1), (-30.49, FRONT, "gather", 0), (-28.49, FRONT, "gather", 2),
             (-26.87, FRONT, "gather", 3), (-24.06, FRONT, "domain", 0), (-23.06, FRONT, "domain", 1),
             (-22.06, FRONT, "domain", 2), (-20.06, FRONT, "domain", 3), (10, BACK, "bias", 0)]
PE_SETUP = [(5.52, "w_t", 0), (6.02, "w_t", 1)]
ACT_SETUP = [(5.03, "w_round", 0), (6, "w_hi", 0), (8.35, "bo_hi", 0), (8.52, "w_mid", 0), (12.51, "bo_mid", 0),
             (13.66, "bo_lo", 0)]
DVE_SETUP = [(2.84, "w_amax", 0), (5, "w_deq", 0), (6.56, "w_res", 0), (10, "w_lo", 0), (11, "bo_less", 0),
             (13, "bo_less2", 0)]


def calendar(plan, setup, lead):
    at = {}
    for phase in range(-1, NC + 1):
        for tau, kind, name, half in plan:
            c = phase + kind
            if 0 <= c < NC:
                when = tau + phase * UNITS + lead
                at.setdefault(int(when // 1), []).append((when, name, c, half))
    for tau, name, half in setup:
        at.setdefault(int(tau + lead), []).append((tau + lead, name, 0, half))
    return {slot: [entry[1:] for entry in sorted(todo)] for slot, todo in at.items()}


def tower_kernel(nc, ids, domain_map, table, w_exp, w_proj, w_q, w_k, w_v, b_q, b_k, b_v, w_o, b_o,
                 static, lam, gam, w_f, b_f, dom_of_col, ident, first_rows, sel_v, sel_y, out):
    pe_at = calendar(PE_PLAN, PE_SETUP, LEAD)
    act_at = calendar(ACT_PLAN, ACT_SETUP, LEAD)
    dve_at = calendar(DVE_PLAN, DVE_SETUP, 0)
    pool_at = calendar(POOL_PLAN, [], 0)
    SLOTS = range(-3 * UNITS, (NC + 1) * UNITS)
    uses = [key for slot in SLOTS for key in pe_at.get(slot, []) if not key[0].startswith("v_less")]
    use = {key: (n % 2, n // 2) for n, key in enumerate(uses)}

    def unit(g):
        c, n = divmod(g, UNITS)
        hg, m = divmod(n, HD)
        return c, n, hg, m % NA, m // NA

    with ExitStack() as ctx:
        def sb(name, shape, dt=F32):
            return ctx.enter_context(nc.sbuf_tensor(name, shape, dt))

        def ps(name, shape, dt=F32):
            return ctx.enter_context(nc.psum_tensor(name, shape, dt))

        def sem(name):
            return ctx.enter_context(nc.semaphore(name))

        ids_sb = sb("ids_sb", [P, NTILE], I32)
        wexp = sb("wexp", [P, KD, NDOM * EXP])
        wproj = sb("wproj", [P, KD, DIM])
        wq = sb("wq", [P, KD, DIM])
        wk = sb("wk", [P, KD, DIM])
        wv = sb("wv", [P, KD, DIM])
        wo = sb("wo", [P, HG, DIM])
        wf = sb("wf", [P, KD, DIM])
        wf_parts = sb("wf_parts", [P, PARTS, KD, DIM], BF16)
        bq = sb("bq", [P, HG])
        bk = sb("bk", [P, HG])
        bk4 = sb("bk4", [P, HG])
        bv = sb("bv", [P, HG])
        bo = sb("bo", [P, DIM])
        bf = sb("bf", [P, DIM])
        wst = sb("wst", [P, HG, P])
        lam_sb = sb("lam_sb", [P, UNITS])
        gam_sb = sb("gam_sb", [P, UNITS])
        domcol = sb("domcol", [P, NDOM * EXP])
        idf = sb("idf", [P, P])
        idb = sb("idb", [P, P], BF16)
        rows32 = sb("rows32", [PARTS * 32, P])
        rows = sb("rows", [PARTS * 32, P], BF16)
        bo_part = sb("bo_part", [P, PARTS - 1, DIM], BF16)
        bo_rows = sb("bo_rows", [PARTS * 32, DIM], BF16)
        neg_idb = sb("neg_idb", [P, P], BF16)
        selv32 = sb("selv32", [P, NB, P])
        selv = sb("selv", [P, NB, P], BF16)
        sely = sb("sely", [P, NB, 32])
        rnd = sb("rnd", [P, 1])
        rnd_neg = sb("rnd_neg", [P, 1])
        dom_i = sb("dom_i", [P, NTILE], I32)
        dom_f = sb("dom_f", [P, NTILE])
        tok = sb("tok", [P, NTILE, DIM])
        emb_t = sb("emb_t", [P, KD, T])
        act_t = sb("act_t", [P, KD, T])
        masked = sb("masked", [P, TT, DIM])
        tmp_f = sb("tmp_f", [P, TT, DIM])
        tmp_b = sb("tmp_b", [P, TT, DIM])
        xq = sb("xq", [P, TT, DIM], BF16)
        xq_t = sb("xq_t", [P, KD, T], BF16)
        kk = sb("kk", [P, 2, HG, T])
        q_sb = sb("q_sb", [P, HG, T])
        v_part = [sb(f"v_part{p}", [P, HG, T], BF16) for p in range(PARTS)]
        v_rows = sb("v_rows", [PARTS * 32, 2, HG, NA, T], BF16)
        y_t = sb("y_t", [P, HG, T])
        vg = sb("vg", [P, NVG, T])
        uu = sb("uu", [P, NU, T])
        carry = sb("carry", [P, UNITS])
        zz = sb("zz", [P, NZ, T])
        bn = sb("bn", [P, 2, TT, 6])
        mv = sb("mv", [P, 2, TT, 2])
        ve = sb("ve", [P, 2, TT])
        sd = sb("sd", [P, 2, TT])
        nr = sb("nr", [P, 2, 4, TT])
        rstd = sb("rstd", [P, 2, TT])
        nmr = sb("nmr", [P, 2, TT])
        am = sb("am", [P, TT])
        xs = sb("xs", [P, TT])
        xinv = sb("xinv", [P, TT])
        wam = sb("wam", [P, KD])
        ws = sb("ws", [P, KD])
        winv = sb("winv", [P, KD])

        vr_ps = ps("vr_ps", [P, NVR, T])
        q_ps = ps("q_ps", [P, HG, T])
        y_ps = ps("y_ps", [P, T])
        scr = ps("scr", [P, 2, T])
        r_ps = ps("r_ps", [P, T])
        scr_two = [scr[:, i, :].rearrange("p (b d) -> p b d", b=2) for i in range(2)]
        scr_bf = [scr[:, i, 0:T // 2].bitcast(BF16).rearrange("p (k t) -> p k t", k=KD) for i in range(2)]

        s_ids = sem("s_ids")
        s_w_tok, s_w_tok2, s_w_qkv, s_w_unit, s_w_back = (sem(n) for n in ("s_w_tok", "s_w_tok2", "s_w_qkv", "s_w_unit", "s_w_back"))
        s_base = [[sem(f"s_base{c}_{h}") for h in range(2)] for c in range(NC)]
        s_dom = [sem(f"s_dom{c}") for c in range(NC)]
        s_const = sem("s_const")
        s_cast = sem("s_cast")
        s_sig = sem("s_sig")
        s_ret = sem("s_ret")
        s_full = [sem("s_full0"), sem("s_full1")]
        s_free = [sem("s_free0"), sem("s_free1")]
        s_var = [sem("s_var1"), sem("s_var2")]
        s_sqrt = [sem("s_sqrt1"), sem("s_sqrt2")]
        s_rstd = [sem("s_rstd1"), sem("s_rstd2")]
        s_xhat = [sem("s_xhat1"), sem("s_xhat2")]
        s_vleft = [sem("s_vleft0"), sem("s_vleft1")]
        s_vpart = [sem("s_vhi"), sem("s_vmid")]
        s_vrows = [sem(f"s_vrows{p}") for p in range(PARTS)]
        s_amax = sem("s_amax")
        s_round = sem("s_round")
        s_xq = sem("s_xq")
        s_h2b = sem("s_h2b")
        s_stored = sem("s_stored")
        s_vr = sem("s_vr")
        s_vg = sem("s_vg")
        s_u = sem("s_u")
        s_scan = sem("s_scan")
        s_carry = sem("s_carry")
        s_z = sem("s_z")
        s_y = sem("s_y")
        s_yt = sem("s_yt")
        s_bo = sem("s_bo")
        s_wq = sem("s_wq")
        s_dve = sem("s_dve")

        def filled(eng, name, c, h):
            bank, before = use[name, c, h]
            eng.wait_ge(s_full[bank], before + 1)
            return bank

        def taken(eng, name, c, h):
            bank, before = use[name, c, h]
            eng.wait_ge(s_free[bank], before + 1)

        block = ctx.enter_context(nc.Block())

        @block.sync
        def _(sp):
            sp.dma_start(ids_sb[:], ids).then_inc(s_ids, 16)
            for dst, src in ((idf, ident), (wexp, w_exp), (domcol, dom_of_col)):
                sp.dma_start(dst[:], src).then_inc(s_w_tok, 16)
            sp.dma_start(wproj[:], w_proj).then_inc(s_w_tok2, 16)
            for dst, src in ((wv, w_v), (bv, b_v), (wk, w_k), (bk, b_k), (wq, w_q), (bq, b_q)):
                sp.dma_start(dst[:], src).then_inc(s_w_qkv, 16)
            for dst, src in ((lam_sb, lam), (gam_sb, gam), (wst, static), (selv32, sel_v), (sely, sel_y)):
                sp.dma_start(dst[:], src).then_inc(s_w_unit, 16)
            for dst, src in ((wf, w_f), (wo, w_o), (bo, b_o), (rows32, first_rows), (bf, b_f)):
                sp.dma_start(dst[:], src).then_inc(s_w_back, 16)
            out_v = out.rearrange("b (c t p) d -> (b c) p t d", c=2 * SEQ // T, p=P)

            def move_v(c):
                if c >= 2:
                    sp.wait_ge(s_vr, UNITS * (c - 1))
                for p in range(PARTS):
                    if p < PARTS - 1:
                        sp.wait_ge(s_vpart[p], HG * (c + 1))
                    else:
                        taken(sp, "v", c, 0)
                        taken(sp, "v", c, 1)
                    for a in range(NA):
                        sp.dma_start(v_rows[32 * p:32 * p + 32, c % 2, :, a, :],
                                     v_part[p][32 * a:32 * a + 32, :, :]).then_inc(s_vrows[p], 16)

            def store(c):
                for h in range(2):
                    taken(sp, "ffn", c, h)
                    sp.dma_start(out_v[2 * c + h], tok[:, TT * c + 2 * h:TT * c + 2 * h + 2, :]).then_inc(s_stored, 16)

            move_v(0)
            for c in range(1, NC):
                if c >= 2:
                    store(c - 2)
                move_v(c)
            store(NC - 2)
            store(NC - 1)
            sp.wait_ge(s_stored, 16 * 2 * NC)

        @block.gpsimd
        def _(pool):
            pool.wait_ge(s_ids, 16)

            def gather(c, t):
                ix = bass.IndirectOffsetOnAxis(ap=ids_sb[:, TT * c + t:TT * c + t + 1], axis=0)
                pool.indirect_dma_start(tok[:, TT * c + t, :], None, table, ix).then_inc(s_base[c][t // 2], 16)

            def domain(c, t):
                ix = bass.IndirectOffsetOnAxis(ap=ids_sb[:, TT * c + t:TT * c + t + 1], axis=0)
                pool.indirect_dma_start(dom_i[:, TT * c + t:TT * c + t + 1], None, domain_map, ix)\
                    .then_inc(s_dom[c], 16)

            def bias(c, _):
                pool.wait_ge(s_xhat[1], 2 * c + 2)
                if c == 0:
                    pool.wait_ge(s_w_back, 80)
                h = tok[:, TT * c:TT * c + TT, :]
                pool.tensor_tensor(h, h, bf[:].rearrange("p (o d) -> p o d", o=1).to_broadcast([P, TT, DIM]),
                                   ALU.add).then_inc(s_h2b, 1)

            stage = {"gather": gather, "domain": domain, "bias": bias}
            for slot in SLOTS:
                if 0 <= slot < NC * UNITS:
                    c, n, hg, a, b = unit(slot)
                    if n == 0:
                        taken(pool, "k", c, 0)
                        taken(pool, "k", c, 1)
                    pool.wait_ge(s_vg, slot + 1)
                    if slot >= NU:
                        pool.wait_ge(s_scan, slot - NU + 1)
                    pool.tensor_tensor(uu[:, slot % NU, :], vg[:, slot % NVG, :], kk[:, c % 2, hg, :],
                                       ALU.mult).then_inc(s_u, 1)
                for name, c, h in pool_at.get(slot, []):
                    stage[name](c, h)

        @block.scalar
        def _(act):
            act.wait_ge(s_w_tok, 48)
            act.activation(idb[:], idf[:], ACT.Copy).then_inc(s_cast, 1)
            act.wait_ge(s_w_unit, 80)
            act.activation(lam_sb[:], lam_sb[:], ACT.Sigmoid).then_inc(s_sig, 1)
            act.activation(selv[:], selv32[:], ACT.Copy)
            act.activation(neg_idb[:], idf[:], ACT.Copy, scale=-1.0).then_inc(s_cast, 1)
            act.wait_ge(s_w_tok2, 16)
            act.activation(wproj[:], wproj[:], ACT.Copy, scale=0.1).then_inc(s_cast, 1)
            act.wait_ge(s_w_qkv, 96)
            act.activation(bk4[:], bk[:], ACT.Copy, scale=0.25).then_inc(s_cast, 1)
            act.wait_ge(s_cast, 4)

            def evacuate(name, dst, reader):
                def step(c, h):
                    bank = filled(act, name, c, h)
                    if c >= 1 and reader:
                        filled(act, reader[0], c - 1, h if reader[1] is None else reader[1])
                    act.activation(dst[:, :, T // 2 * h:T // 2 * (h + 1)], scr_two[bank], ACT.Copy)\
                       .then_inc(s_free[bank], 1)
                return step

            def residual(name):
                def step(c, h):
                    bank = filled(act, name, c, h)
                    act.activation(tok[:, TT * c + 2 * h:TT * c + 2 * h + 2, :], scr_two[bank], ACT.Copy)\
                       .then_inc(s_free[bank], 1)
                return step

            def q(c, hg):
                bank = filled(act, "q", c, hg)
                if c >= 1:
                    act.wait_ge(s_y, (UNITS * (c - 1) + HD * (hg + 1)) // NA)
                act.activation(q_sb[:, hg, :], scr[:, bank, :], ACT.Identity, bias=bq[:, hg:hg + 1])
                act.activation(q_ps[:, hg, :], scr[:, bank, :], ACT.Identity, bias=bq[:, hg:hg + 1])\
                   .then_inc(s_free[bank], 1)

            def v_part_of(p):
                def step(c, hg):
                    bank = filled(act, "v", c, hg)
                    if p:
                        act.wait_ge(s_vleft[p - 1], HG * c + hg + 1)
                    if c >= 1 and hg == 0:
                        act.wait_ge(s_vrows[p], 16 * NA * c)
                        if c == 1:
                            act.wait_ge(s_vr, HD)
                    act.activation(v_part[p][:, hg, :], scr[:, bank, :], ACT.Identity, bias=bv[:, hg:hg + 1])\
                       .then_inc(s_free[bank] if p == PARTS - 1 else s_vpart[p], 1)
                return step

            def k(c, hg):
                bank = filled(act, "k", c, hg)
                if c >= 2:
                    act.wait_ge(s_u, UNITS * (c - 1))
                act.activation(kk[:, c % 2, hg, :], scr[:, bank, :], ACT.Identity, bias=bk4[:, hg:hg + 1],
                               scale=HD ** -0.5).then_inc(s_free[bank], 1)

            def y(c, hg):
                act.wait_ge(s_y, (UNITS * c + HD * (hg + 1)) // NA)
                if c >= 1:
                    filled(act, "attn", c - 1, 1)
                act.activation(y_t[:, hg, :], y_ps[:], ACT.Copy).then_inc(s_yt, 1)

            def sqrt(n):
                def step(c, h):
                    act.wait_ge(s_var[n], 2 * c + h + 1)
                    two = slice(2 * h, 2 * h + 2)
                    act.activation(sd[:, n, two], ve[:, n, two], ACT.Sqrt).then_inc(s_sqrt[n], 1)
                return step

            def xhat(n, dst):
                def step(c, h):
                    if n == 0 and c >= 1:
                        filled(act, "xhat_t", c - 1, h)
                    act.wait_ge(s_rstd[n], 2 * c + h + 1)
                    for t in (2 * h, 2 * h + 1):
                        last = act.activation(dst[:, t, :], tok[:, TT * c + t, :], ACT.Identity,
                                              bias=nmr[:, n, t:t + 1], scale=rstd[:, n, t:t + 1])
                    last.then_inc(s_xhat[n], 1)
                return step

            def quant(c, h):
                act.wait_ge(s_amax, 2 * c + h + 1)
                for t in (2 * h, 2 * h + 1):
                    last = act.activation(tmp_b[:, t, :], tmp_b[:, t, :], ACT.Identity, bias=rnd[:],
                                          scale=xinv[:, t:t + 1])
                last.then_inc(s_round, 1)
                act.wait_ge(s_round, 2 * c + h + 1)
                if c >= 1:
                    filled(act, "xq_t", c - 1, h)
                two = slice(2 * h, 2 * h + 2)
                act.activation(xq[:, two, :], tmp_b[:, two, :], ACT.Identity, bias=rnd_neg[:]).then_inc(s_xq, 1)

            def xq_evac(c, h):
                bank = filled(act, "xq_t", c, h)
                if c >= 1:
                    filled(act, "ffn", c - 1, h)
                act.activation(xq_t[:, :, T // 2 * h:T // 2 * (h + 1)], scr_bf[bank], ACT.Copy)\
                   .then_inc(s_free[bank], 1)

            def bo_hi(*_):
                act.wait_ge(s_w_back, 80)
                act.activation(rows[:], rows32[:], ACT.Copy)
                act.activation(bo_part[:, 0, :], bo[:], ACT.Copy).then_inc(s_bo, 1)

            def bo_mid(*_):
                act.wait_ge(s_bo, 2)
                act.activation(bo_rows[0:32, :], bo_part[0:32, 0, :], ACT.Copy)
                act.activation(bo_rows[32:64, :], bo[32:64, :], ACT.Copy)
                act.activation(bo_part[:, 1, :], bo[:], ACT.Copy).then_inc(s_bo, 1)

            def bo_lo(*_):
                act.wait_ge(s_bo, 4)
                act.activation(bo_rows[64:96, :], bo[64:96, :], ACT.Copy).then_inc(s_bo, 1)

            def w_round(*_):
                act.wait_ge(s_wq, 1)
                for k_ in range(KD):
                    last = act.activation(wf[:, k_, :], wf[:, k_, :], ACT.Identity, bias=rnd[:],
                                          scale=winv[:, k_:k_ + 1])
                last.then_inc(s_wq, 1)

            def w_hi(*_):
                for k_ in range(KD):
                    bank = filled(act, "w_t", 0, k_)
                    last = act.activation(wf_parts[:, 0, k_, :], scr[:, bank, 0:DIM], ACT.Copy)
                last.then_inc(s_wq, 1)

            def w_mid(*_):
                taken(act, "w_t", 0, 0)
                taken(act, "w_t", 0, 1)
                act.activation(wf_parts[:, 1], wf[:], ACT.Copy).then_inc(s_wq, 1)

            stage = {"base_t": evacuate("base_t", emb_t, ("corr", None)), "masked_t": evacuate("masked_t", emb_t, None),
                     "xhat_t": evacuate("xhat_t", act_t, ("q", 1)),
                     "corr": residual("corr"), "attn": residual("attn"),
                     "q": q, "v_hi": v_part_of(0), "v_mid": v_part_of(1), "v_lo": v_part_of(2), "k": k, "y": y, "sqrt1": sqrt(0),
                     "sqrt2": sqrt(1), "xhat": xhat(0, tmp_f), "xhat2": xhat(1, tmp_b), "quant": quant,
                     "xq_t": xq_evac, "w_round": w_round, "bo_hi": bo_hi, "bo_mid": bo_mid, "bo_lo": bo_lo, "w_hi": w_hi, "w_mid": w_mid}
            for slot in SLOTS:
                if 0 <= slot < NC * UNITS:
                    act.wait_ge(s_vr, slot + 1)
                    if slot >= NVG:
                        act.wait_ge(s_u, slot - NVG + 1)
                    n = slot % UNITS
                    act.activation(vg[:, slot % NVG, :], vr_ps[:, slot % NVR, :], ACT.Copy,
                                   scale=gam_sb[:, n:n + 1]).then_inc(s_vg, 1)
                for name, c, h in act_at.get(slot, []):
                    stage[name](c, h)

        @block.vector
        def _(dve):
            chain = [0]
            saved = {}

            def link(ins):
                chain[0] += 1
                ins.then_inc(s_dve, 1)
                dve.wait_ge(s_dve, chain[0])

            dve.memset(rnd[:], ROUND)
            dve.memset(rnd_neg[:], -ROUND).then_inc(s_const, 1)
            dve.wait_ge(s_sig, 1)
            dve.tensor_scalar(r_ps[:, 0:UNITS], lam_sb[:], -1.0, 1.0, ALU.mult, ALU.add).then_inc(s_ret, 1)

            def mask(c, h):
                if h == 0:
                    dve.wait_ge(s_dom[c], 16 * TT)
                    link(dve.tensor_copy(dom_f[:, TT * c:TT * c + TT], dom_i[:, TT * c:TT * c + TT]))
                bank = filled(dve, "expand", c, h)
                if c >= 1:
                    filled(dve, "masked_t", c - 1, h)
                for i in range(2):
                    t = 2 * h + i
                    last = dve.scalar_tensor_tensor(masked[:, t, :], domcol[:], dom_f[:, TT * c + t:TT * c + t + 1],
                                                    scr_two[bank][:, i, :], ALU.is_equal, ALU.mult)
                last.then_inc(s_free[bank], 1)

            def stats(n, name):
                def step(c, h):
                    taken(dve, name, c, h)
                    for t in (2 * h, 2 * h + 1):
                        last = dve.bn_stats(bn[:, n, t, :], tok[:, TT * c + t, :])
                    link(last)
                    for t in (2 * h, 2 * h + 1):
                        last = dve.bn_aggr(mv[:, n, t, :], bn[:, n, t, :])
                    link(last)
                    two = slice(2 * h, 2 * h + 2)
                    dve.tensor_scalar(ve[:, n, two], mv[:, n, two, 1], LNEPS, None, ALU.add).then_inc(s_var[n], 1)
                return step

            def rsqrt(n):
                def step(c, h):
                    dve.wait_ge(s_sqrt[n], 2 * c + h + 1)
                    two = slice(2 * h, 2 * h + 2)
                    r0, sq, vs, fix = (nr[:, n, i, two] for i in range(4))
                    link(dve.reciprocal(r0, sd[:, n, two]))
                    link(dve.tensor_tensor(sq, r0, r0, ALU.mult))
                    link(dve.tensor_tensor(vs, sq, ve[:, n, two], ALU.mult))
                    link(dve.tensor_scalar(fix, vs, -0.5, 1.5, ALU.mult, ALU.add))
                    link(dve.tensor_tensor(rstd[:, n, two], r0, fix, ALU.mult))
                    dve.scalar_tensor_tensor(nmr[:, n, two], mv[:, n, two, 0], -1.0, rstd[:, n, two], ALU.mult,
                                             ALU.mult).then_inc(s_rstd[n], 1)
                return step

            def amax(c, h):
                dve.wait_ge(s_xhat[1], 2 * c + h + 1)
                two = slice(2 * h, 2 * h + 2)
                link(dve.tensor_reduce(am[:, two], tmp_b[:, two, :], AX.X, ALU.max, apply_absolute_value=True))
                link(dve.tensor_scalar(xs[:, two], am[:, two], QEPS, 1.0 / QMAX, ALU.max, ALU.mult))
                dve.reciprocal(xinv[:, two], xs[:, two]).then_inc(s_amax, 1)

            def finish(c, h):
                bank = filled(dve, "ffn", c, h)
                if h == 0:
                    dve.wait_ge(s_h2b, c + 1)
                for i in range(2):
                    t = 2 * h + i
                    x = tok[:, TT * c + t, :]
                    last = dve.scalar_tensor_tensor(x, scr_two[bank][:, i, :], xs[:, t:t + 1], x, ALU.mult, ALU.add)
                last.then_inc(s_free[bank], 1)

            def bo_less(*_):
                dve.wait_ge(s_bo, 1)
                dve.tensor_tensor(bo[:], bo[:], bo_part[:, 0, :], ALU.subtract).then_inc(s_bo, 1)

            def bo_less2(*_):
                dve.wait_ge(s_bo, 3)
                dve.tensor_tensor(bo[:], bo[:], bo_part[:, 1, :], ALU.subtract).then_inc(s_bo, 1)

            def w_amax(*_):
                dve.wait_ge(s_w_back, 80)
                link(dve.tensor_reduce(wam[:], wf[:], AX.X, ALU.max, apply_absolute_value=True))
                link(dve.tensor_scalar(ws[:], wam[:], QEPS, 1.0 / QMAX, ALU.max, ALU.mult))
                dve.reciprocal(winv[:], ws[:]).then_inc(s_wq, 1)

            def w_deq(*_):
                dve.wait_ge(s_wq, 2)
                for k_ in range(KD):
                    last = dve.tensor_scalar(wf[:, k_, :], wf[:, k_, :], -ROUND, ws[:, k_:k_ + 1], ALU.add, ALU.mult)
                last.then_inc(s_wq, 1)

            def w_res(*_):
                dve.wait_ge(s_wq, 4)
                for k_ in range(KD):
                    bank = filled(dve, "w_t", 0, k_)
                    dve.tensor_tensor(wf[:, k_, :], scr[:, bank, 0:DIM], wf_parts[:, 0, k_, :], ALU.subtract)\
                       .then_inc(s_free[bank], 1)

            def w_lo(*_):
                dve.wait_ge(s_wq, 5)
                dve.tensor_tensor(wf_parts[:, 2], wf[:], wf_parts[:, 1], ALU.subtract).then_inc(s_wq, 1)

            def scan(g):
                c, n, hg, a, b = unit(g)
                dve.wait_ge(s_u, g + 1)
                if g >= NZ:
                    dve.wait_ge(s_y, (g - NZ) // NA + 1)
                start = 0.0 if c % (SEQ // T) == 0 else carry[:, n:n + 1]
                dve.tensor_tensor_scan(zz[:, g % NZ, :], r_ps[:, n:n + 1].to_broadcast([P, T]), uu[:, g % NU, :],
                                       start, ALU.mult, ALU.add).then_inc(s_scan, 1)

            def keep(g):
                c, n, hg, a, b = unit(g)
                if (c + 1) % (SEQ // T):
                    saved[g] = len(saved) + 1
                    dve.wait_ge(s_scan, g + 2)
                    dve.tensor_copy(carry[:, n:n + 2], zz[:, g % NZ:g % NZ + 2, T - 1]).then_inc(s_carry, 1)

            def product(g):
                c, n, hg, a, b = unit(g)
                if n % HD == 0:
                    taken(dve, "q", c, hg)
                dve.wait_ge(s_scan, g + 2)
                x = zz[:, g % NZ:g % NZ + 2, :]
                if (c + 1) % (SEQ // T):
                    dve.wait_ge(s_carry, saved[g])
                q = q_ps[:, hg, :].rearrange("p (o t) -> p o t", o=1).to_broadcast([P, 2, T])
                dve.tensor_tensor(x, x, q, ALU.mult).then_inc(s_z, 1)

            stage = {"mask": mask, "stat1": stats(0, "corr"), "rstd1": rsqrt(0), "stat2": stats(1, "attn"),
                     "rstd2": rsqrt(1), "amax": amax, "out": finish, "w_amax": w_amax, "bo_less": bo_less, "bo_less2": bo_less2, "w_deq": w_deq,
                     "w_res": w_res, "w_lo": w_lo}
            dve.wait_ge(s_w_tok, 48)
            for slot in SLOTS:
                if 2 < slot <= NC * UNITS + 1 and slot % 2:
                    keep(slot - 3)
                if 0 <= slot < NC * UNITS:
                    if slot == 0:
                        dve.wait_ge(s_ret, 1)
                    scan(slot)
                if 2 < slot <= NC * UNITS + 1 and slot % 2:
                    product(slot - 3)
                for name, c, h in dve_at.get(slot, []):
                    stage[name](c, h)

        @block.tensor
        def _(pe):
            def scratch(name, c, h):
                bank, before = use[name, c, h]
                if before:
                    pe.wait_ge(s_free[bank], before)
                return bank

            def transposes(name, src, wait, ident_, view):
                def step(c, h):
                    bank = scratch(name, c, h)
                    wait(c, h)
                    for i in range(2):
                        for k_ in range(KD):
                            last = pe.transpose(view[bank][:, k_, P * i:P * i + P],
                                                src(c, 2 * h + i)[:, P * k_:P * k_ + P], ident_[:])
                    last.then_inc(s_full[bank], 1)
                return step

            def token_major(name, weight):
                def step(c, h):
                    bank = scratch(name, c, h)
                    if (name, c, h) == ("corr", 0, 0):
                        pe.wait_ge(s_cast, 3)
                    for i in range(2):
                        t = 2 * h + i
                        for k_ in range(KD):
                            last = pe.matmul(scr_two[bank][:, i, :], emb_t[:, k_, P * t:P * t + P], weight[:, k_, :],
                                             start=(k_ == 0), stop=(k_ == KD - 1 and name == "expand"))
                        if name == "corr":
                            last = pe.matmul(scr_two[bank][:, i, :], idf[:], tok[:, TT * c + t, :], start=False, stop=True)
                    last.then_inc(s_full[bank], 1)
                return step

            def channel_major(name, weight):
                def step(c, hg):
                    bank = scratch(name, c, hg)
                    if c == 0:
                        pe.wait_ge(s_w_qkv, 96)
                    for k_ in range(KD):
                        last = pe.matmul(scr[:, bank, :], weight[:, k_, P * hg:P * hg + P], act_t[:, k_, :],
                                         start=(k_ == 0), stop=(k_ == KD - 1))
                    last.then_inc(s_full[bank], 1)
                return step

            def v(c, hg):
                bank = scratch("v", c, hg)
                if c == 0:
                    pe.wait_ge(s_w_qkv, 96)
                for k_ in range(KD):
                    last = pe.matmul(scr[:, bank, :], wv[:, k_, P * hg:P * hg + P], act_t[:, k_, :],
                                     start=(k_ == 0), stop=(k_ == KD - 1))
                last.then_inc(s_full[bank], 1)

            def v_less(p):
                def step(c, hg):
                    bank, _ = use["v", c, hg]
                    pe.wait_ge(s_vpart[p], HG * c + hg + 1)
                    pe.matmul(scr[:, bank, :], neg_idb[:], v_part[p][:, hg, :], start=False, stop=True,
                              skip_group_check=True).then_inc(s_vleft[p], 1)
                return step

            def attn(c, h):
                bank = scratch("attn", c, h)
                pe.wait_ge(s_yt, HG * (c + 1))
                if c == 0:
                    pe.wait_ge(s_w_back, 80)
                    pe.wait_ge(s_bo, 5)
                for i in range(2):
                    t = 2 * h + i
                    x = scr_two[bank][:, i, :]
                    pe.matmul(x, rows[:], bo_rows[:], start=True, stop=False)
                    pe.matmul(x, idf[:], tok[:, TT * c + t, :], start=False, stop=False)
                    for hg in range(HG):
                        last = pe.matmul(x, y_t[:, hg, P * t:P * t + P], wo[:, hg, :],
                                         start=False, stop=(hg == HG - 1))
                last.then_inc(s_full[bank], 1)

            def ffn(c, h):
                bank = scratch("ffn", c, h)
                if c == 0:
                    pe.wait_ge(s_wq, 6)
                taken(pe, "xq_t", c, h)
                for i in range(2):
                    t = 2 * h + i
                    for n in range(PARTS * KD):
                        p, k_ = n // KD, n % KD
                        last = pe.matmul(scr_two[bank][:, i, :], xq_t[:, k_, P * t:P * t + P], wf_parts[:, p, k_, :],
                                         start=(n == 0), stop=(n == PARTS * KD - 1))
                last.then_inc(s_full[bank], 1)

            def w_t(_, k_):
                bank = scratch("w_t", 0, k_)
                pe.wait_ge(s_wq, 3)
                for o in range(KD):
                    last = pe.transpose(scr[:, bank, P * o:P * o + P], wf[:, o, P * k_:P * k_ + P], idf[:])
                last.then_inc(s_full[bank], 1)

            stage = {"base_t": transposes("base_t", lambda c, t: tok[:, TT * c + t, :],
                                          lambda c, h: pe.wait_ge(s_base[c][h], 16 * 2), idf, scr_two),
                     "expand": token_major("expand", wexp),
                     "masked_t": transposes("masked_t", lambda c, t: masked[:, t, :],
                                            lambda c, h: taken(pe, "expand", c, h), idf, scr_two),
                     "corr": token_major("corr", wproj),
                     "xhat_t": transposes("xhat_t", lambda c, t: tmp_f[:, t, :],
                                          lambda c, h: pe.wait_ge(s_xhat[0], 2 * c + h + 1), idf, scr_two),
                     "v": v, "v_less": v_less(0), "v_less2": v_less(1), "k": channel_major("k", wk), "q": channel_major("q", wq),
                     "xq_t": transposes("xq_t", lambda c, t: xq[:, t, :], lambda c, h: pe.wait_ge(s_xq, 2 * c + h + 1),
                                        idb, scr_bf),
                     "attn": attn, "ffn": ffn, "w_t": w_t}
            operand = {"expand": "base_t", "corr": "masked_t", "v": "xhat_t", "k": "xhat_t", "q": "xhat_t"}

            def spread(g):
                c, n, hg, a, b = unit(g)
                if n % HD == 0 and g > 0:
                    for p in range(PARTS):
                        pe.wait_ge(s_vrows[p], 16 * NA * (c + 1))
                if g >= NVR:
                    pe.wait_ge(s_vg, g - NVR + 1)
                if g < HD:
                    if g == 0:
                        taken(pe, "v", 0, 0)
                    rows_a = slice(32 * a, 32 * a + 32)
                    for p in range(PARTS):
                        last = pe.matmul(vr_ps[:, g % NVR, :], selv[rows_a, b, :], v_part[p][rows_a, 0, :],
                                         start=(p == 0), stop=(p == PARTS - 1))
                    last.then_inc(s_vr, 1)
                    return
                pe.matmul(vr_ps[:, g % NVR, :], selv[0:PARTS * 32, b, :], v_rows[:, c % 2, hg, a, :], start=True, stop=True)\
                  .then_inc(s_vr, 1)

            def collect(g):
                c, n, hg, a, b = unit(g)
                if n % HD == 0 and g > 0:
                    pe.wait_ge(s_yt, g // HD)
                if b == 0:
                    taken(pe, "q", c, hg)
                    pe.matmul(y_ps[:], wst[:, hg, :], q_sb[:, hg, :], start=True, stop=True)
                pe.wait_ge(s_z, (g + NA) // 2)
                for a in range(NA):
                    last = pe.matmul(y_ps[32 * a:32 * a + 32, :], sely[:, b, :], zz[:, (g + a) % NZ, :],
                                     start=False, stop=True, skip_group_check=True)
                last.then_inc(s_y, 1)

            pe.wait_ge(s_w_tok, 48)
            for slot in SLOTS:
                if slot == 0:
                    pe.wait_ge(s_cast, 4)
                if 0 <= slot < NC * UNITS:
                    spread(slot)
                g = slot - LAG - NA + 1
                if g >= 0 and g % NA == 0 and g < NC * UNITS:
                    collect(g)
                for name, c, h in pe_at.get(slot, []):
                    if name in ("v", "k", "q"):
                        taken(pe, operand[name], c, 0)
                        taken(pe, operand[name], c, 1)
                    elif name in operand:
                        taken(pe, operand[name], c, h)
                    stage[name](c, h)


def kernel(**inputs):
    import concourse.bacc as _bacc
    from concourse.bass_utils import run_bass_kernel_spmd as _run

    def halves(m):
        return m.reshape(KD, P, -1).transpose(1, 0, 2)

    g = {k: np.asarray(v) for k, v in inputs.items()}
    rows = np.arange(DIM).reshape(HG, P // HD, NA, NB).transpose(0, 2, 1, 3).reshape(-1)
    w_qkv, b_qkv = g["L0_attn_Wqkv_w"], g["L0_attn_Wqkv_b"]

    def per_unit(m):
        m = m.reshape(HG, P // HD, NA, NB, HD).transpose(1, 4, 0, 3, 2)
        return m.reshape(P, UNITS)

    h8 = np.arange(P) // HD
    sel_v = np.zeros((NA, P // HD, NB, NB, P), np.float32)
    sel_y = np.zeros((P, NB, P // HD, NB), np.float32)
    for b in range(NB):
        for h in range(P // HD):
            sel_v[:, h, b, b, h8 == h] = 1.0
            sel_y[h8 == h, b, h, b] = 1.0
    first_rows = np.zeros((PARTS * 32, P), np.float32)
    first_rows[::32] = 1.0
    static = np.zeros((P // HD, HD, HG, NA, P // HD, NB), np.float32)
    w = g["L0_attn_W_static"].reshape(HG, P // HD, NA, NB, HD)
    for h in range(P // HD):
        static[h, :, :, :, h, :] = w[:, h].transpose(3, 0, 1, 2)
    static = static.reshape(P, HG, P)
    arrays = {
        "ids": g["x"].reshape(NTILE, P).T,
        "domain_map": g["L0_tok_domain_map"].reshape(-1, 1),
        "table": g["L0_tok_emb_table"],
        "w_exp": halves(g["L0_tok_W_exp"].reshape(NDOM * EXP, DIM).T),
        "w_proj": halves(g["L0_tok_W_proj"].transpose(0, 2, 1).reshape(NDOM * EXP, DIM)),
        "w_q": halves(w_qkv[:DIM].T),
        "w_k": halves(w_qkv[DIM:2 * DIM].T),
        "w_v": halves(w_qkv[2 * DIM:][rows].T),
        "b_q": b_qkv[:DIM].reshape(HG, P).T,
        "b_k": b_qkv[DIM:2 * DIM].reshape(HG, P).T,
        "b_v": b_qkv[2 * DIM:][rows].reshape(HG, P).T,
        "w_o": halves(g["L0_attn_out_w"].T[rows]),
        "b_o": np.broadcast_to(g["L0_attn_out_b"], (P, DIM)),
        "static": static,
        "lam": per_unit(g["L0_attn_Lambda_raw"]),
        "gam": per_unit(g["L0_attn_Gamma"]),
        "w_f": halves(g["L0_ffn_weight"]),
        "b_f": np.broadcast_to(g["L0_ffn_bias"], (P, DIM)),
        "dom_of_col": np.broadcast_to(np.arange(NDOM * EXP, dtype=np.float32) // EXP, (P, NDOM * EXP)),
        "ident": np.eye(P, dtype=np.float32),
        "first_rows": first_rows,
        "sel_v": sel_v.reshape(P, NB, P),
        "sel_y": sel_y.reshape(P, NB, 32),
    }
    nc = _bacc.Bacc("TRN2", target_bir_lowering=False, num_devices=1)
    args = {}
    for name, a in arrays.items():
        arrays[name] = a = np.ascontiguousarray(a)
        args[name] = nc.dram_tensor(f"in_{name}", a.shape, mybir.dt.from_np(a.dtype), kind="ExternalInput").ap()
    out = nc.dram_tensor("out_h", (BATCH, SEQ, DIM), F32, kind="ExternalOutput").ap()
    tower_kernel(nc, out=out, **args)
    r = _run(nc, [{f"in_{name}": a for name, a in arrays.items()}], core_ids=[0])
    return r.results[0]["out_h"]
```

```python
from contextlib import ExitStack

import numpy as np

import concourse.bass as bass
from concourse import mybir
from concourse.alu_op_type import AluOpType as ALU

F32 = mybir.dt.float32
BF16 = mybir.dt.bfloat16
I32 = mybir.dt.int32
ACT = mybir.ActivationFunctionType
AX = mybir.AxisListType

P = 128
BATCH, SEQ, DIM, HEADS, HD = 2, 1024, 256, 16, 16
TOKENS = BATCH * SEQ
NTILE = TOKENS // P
T = 512
TT = T // P
NC = TOKENS // T
KD = DIM // P
HG = HEADS * HD // P
UNITS = HG * HD
NB = 4
NA = HD // NB
PARTS = 3
NDOM, EXP = 8, 32
ROUND = 12582912.0
QMAX, QEPS, LNEPS = 127.0, 1e-8, 1e-5

DIRECT = 4
WAKE = 10
LAG = 10
LEAD = 4
NVR, NVG, NU, NZ = 2, 8, 8, 16

PE_CALENDAR = """
    -1: base_t 0.0, expand 0.0, wake 0.8, base_t 0.1, masked_t 0.0, expand 0.1, corr 0.0, masked_t 0.1, corr 0.1,
    xhat_t 0.0, wake 0.10, xhat_t 0.1, v 0.0, v 0.1, v_less 0.0, v_less 0.1, v_less2 0.0; 0: v_less2 0.1, k 0.0,
    k 0.1; 2: q 0.0; 3: q 0.1; 5: w_t 0.0, w_t 0.1; 8: base_t 1.0, base_t 1.1; 10: expand 1.0; 12: expand 1.1,
    masked_t 1.0; 13: masked_t 1.1, corr 1.0; 15: corr 1.1; 17: xhat_t 1.0; 23: xhat_t 1.1; 26: v 1.0; 27: v 1.1,
    v_less 1.0; 29: v_less2 1.0, v_less 1.1; 31: k 1.0, v_less2 1.1; 33: k 1.1; 34: q 1.0; 35: q 1.1;
    40: base_t 2.0; 43: base_t 2.1, expand 2.0, attn 0.0, attn 0.1; 46: masked_t 2.0, expand 2.1; 47: corr 2.0,
    masked_t 2.1; 49: xq_t 0.0; 50: corr 2.1, xq_t 0.1; 52: ffn 0.0; 54: ffn 0.1; 56: xhat_t 2.0, xhat_t 2.1;
    58: v 2.0; 59: v 2.1, v_less 2.0; 61: v_less2 2.0; 62: v_less 2.1; 63: k 2.0, v_less2 2.1; 65: k 2.1; 66: q 2.0;
    67: q 2.1; 72: base_t 3.0; 75: base_t 3.1, expand 3.0, attn 1.0, attn 1.1; 78: masked_t 3.0, expand 3.1;
    79: corr 3.0, masked_t 3.1; 81: xq_t 1.0; 82: corr 3.1, xq_t 1.1; 84: ffn 1.0; 86: ffn 1.1; 88: xhat_t 3.0,
    xhat_t 3.1; 90: v 3.0; 91: v 3.1, v_less 3.0; 93: v_less2 3.0, v_less 3.1; 95: k 3.0, v_less2 3.1; 97: k 3.1;
    98: q 3.0; 100: q 3.1; 107: attn 2.0, attn 2.1; 114: xq_t 2.0, ffn 2.0; 118: xq_t 2.1; 120: ffn 2.1;
    130: wake 3.10; 131: wake 3.3; 135: wake 3.6; 137: attn 3.0, attn 3.1, wake 3.20, xq_t 3.0, wake 3.6, ffn 3.0,
    xq_t 3.1, ffn 3.1
"""
ACT_CALENDAR = """
    -1: base_t 0.0, w_scale 0.0, select 0.0, base_t 0.1, masked_t 0.0, corr 0.0, b_scale 0.0, masked_t 0.1,
    sqrt1 0.0, xhat 0.0, corr 0.1, sqrt1 0.1, xhat_t 0.0, xhat 0.1, bo_hi 0.0, w_round 0.0, xhat_t 0.1, bo_mid 0.0,
    bo_lo 0.0, v_hi 0.0, v_hi 0.1, v_mid 0.0, v_mid 0.1, v_lo 0.0, v_lo 0.1; 0: k 0.0; 1: k 0.1; 2: q 0.0; 3: q 0.1;
    5: w_hi 0.0; 7: w_mid 0.0; 8: base_t 1.0, base_t 1.1; 12: masked_t 1.0; 13: masked_t 1.1, corr 1.0;
    15: sqrt1 1.0, xhat 1.0, corr 1.1; 17: xhat_t 1.0; 18: sqrt1 1.1; 21: xhat 1.1; 23: xhat_t 1.1; 25: y 0.0;
    26: v_hi 1.0; 27: v_hi 1.1; 28: v_mid 1.0; 29: v_lo 1.0; 30: v_mid 1.1; 31: k 1.0, v_lo 1.1; 33: k 1.1;
    34: q 1.0; 40: base_t 2.0; 41: q 1.1, y 0.1; 42: base_t 2.1; 43: attn 0.0, sqrt2 0.0, attn 0.1; 44: xhat2 0.0;
    46: sqrt2 0.1, masked_t 2.0, quant 0.0, xhat2 0.1; 47: corr 2.0, masked_t 2.1; 49: quant 0.1, xq_t 0.0,
    sqrt1 2.0; 50: corr 2.1, xq_t 0.1; 52: xhat 2.0, sqrt1 2.1; 54: scaled 0.0, scaled 0.1, xhat 2.1;
    56: xhat_t 2.0, xhat_t 2.1; 58: y 1.0, v_hi 2.0; 60: v_mid 2.0, v_hi 2.1; 61: v_lo 2.0; 62: v_mid 2.1;
    63: k 2.0, v_lo 2.1; 65: k 2.1; 66: q 2.0; 72: base_t 3.0; 73: q 2.1, y 1.1; 74: base_t 3.1; 75: attn 1.0,
    sqrt2 1.0, attn 1.1; 76: xhat2 1.0; 78: sqrt2 1.1, masked_t 3.0, quant 1.0, xhat2 1.1; 79: corr 3.0,
    masked_t 3.1; 81: quant 1.1, xq_t 1.0, sqrt1 3.0; 82: corr 3.1, xq_t 1.1; 84: xhat 3.0, sqrt1 3.1;
    86: scaled 1.0, scaled 1.1, xhat 3.1; 88: xhat_t 3.0, xhat_t 3.1; 90: y 2.0, v_hi 3.0; 91: v_hi 3.1;
    92: v_mid 3.0; 93: v_lo 3.0; 95: v_mid 3.1, k 3.0, v_lo 3.1; 97: k 3.1; 98: q 3.0; 105: q 3.1, y 2.1;
    107: attn 2.0, sqrt2 2.0, attn 2.1; 108: xhat2 2.0; 110: sqrt2 2.1; 112: quant 2.0, xhat2 2.1, xq_t 2.0;
    114: scaled 2.0; 116: quant 2.1; 118: xq_t 2.1; 120: scaled 2.1; 121: y 3.0; 127: y 3.1, attn 3.0, sqrt2 3.0,
    attn 3.1, xhat2 3.0, sqrt2 3.1, quant 3.0, xhat2 3.1, xq_t 3.0, quant 3.1, xq_t 3.1
"""
DVE_CALENDAR = """
    -1: mask 0.0, mask 0.1, stat1 0.0, rstd1 0.0, w_amax 0.0, stat1 0.1, rstd1 0.1, bo_less 0.0, bo_less2 0.0,
    w_deq 0.0; 3: w_res 0.0; 7: mask 1.0; 9: mask 1.1; 13: stat1 1.0, rstd1 1.0; 15: stat1 1.1; 16: rstd1 1.1;
    17: w_lo 0.0; 40: mask 2.0; 42: stat2 0.0; 43: rstd2 0.0, stat2 0.1, amax 0.0, rstd2 0.1, mask 2.1;
    45: amax 0.1, stat1 2.0; 47: rstd1 2.0, stat1 2.1; 49: rstd1 2.1; 72: mask 3.0; 74: stat2 1.0; 75: rstd2 1.0,
    stat2 1.1, amax 1.0, rstd2 1.1, mask 3.1; 77: amax 1.1, stat1 3.0; 79: rstd1 3.0, stat1 3.1; 81: rstd1 3.1;
    105: stat2 2.0; 106: rstd2 2.0; 107: stat2 2.1, amax 2.0, rstd2 2.1; 109: amax 2.1; 129: stat2 3.0, rstd2 3.0,
    stat2 3.1, amax 3.0, rstd2 3.1, amax 3.1, out 3.0, out 3.1
"""
POOL_CALENDAR = """
    46: bias 0.0; 54: out 0.0; 59: out 0.1; 78: bias 1.0; 86: out 1.0; 91: out 1.1; 112: bias 2.0; 127: out 2.0,
    out 2.1, bias 3.0
"""


def calendar(text):
    at = {}
    for entry in text.replace("\n", " ").split(";"):
        slot, stages = entry.split(":")
        at[int(slot)] = []
        for stage in stages.split(","):
            name, where = stage.split()
            chunk, part = where.split(".")
            at[int(slot)].append((name, int(chunk), int(part)))
    return at


def tower_kernel(nc, ids, domain_map, table, w_exp, w_proj, w_q, w_k, w_v, b_q, b_k, b_v, w_o, b_o,
                 static, lam, gam, w_f, b_f, dom_of_col, ident, first_rows, sel_v, sel_y, out):
    pe_at = calendar(PE_CALENDAR)
    act_at = calendar(ACT_CALENDAR)
    dve_at = calendar(DVE_CALENDAR)
    pool_at = calendar(POOL_CALENDAR)
    SLOTS = range(-1, (NC + 1) * UNITS)
    uses = [key for slot in SLOTS for key in pe_at.get(slot, []) if not key[0].startswith(("v_less", "wake"))]
    use = {key: (n % 2, n // 2) for n, key in enumerate(uses)}

    def unit(g):
        c, n = divmod(g, UNITS)
        hg, m = divmod(n, HD)
        return c, n, hg, m % NA, m // NA

    with ExitStack() as ctx:
        def sb(name, shape, dt=F32):
            return ctx.enter_context(nc.sbuf_tensor(name, shape, dt))

        def ps(name, shape, dt=F32):
            return ctx.enter_context(nc.psum_tensor(name, shape, dt))

        def sem(name):
            return ctx.enter_context(nc.semaphore(name))

        ids_sb = sb("ids_sb", [P, NTILE], I32)
        wexp = sb("wexp", [P, KD, NDOM * EXP])
        wproj = sb("wproj", [P, KD, DIM])
        wq = sb("wq", [P, KD, DIM])
        wk = sb("wk", [P, KD, DIM])
        wv = sb("wv", [P, KD, DIM])
        wo = sb("wo", [P, HG, DIM])
        wf = sb("wf", [P, KD, DIM])
        wf_parts = sb("wf_parts", [P, PARTS, KD, DIM], BF16)
        bq = sb("bq", [P, HG])
        bk = sb("bk", [P, HG])
        bk4 = sb("bk4", [P, HG])
        bv = sb("bv", [P, HG])
        bo = sb("bo", [P, DIM])
        bf = sb("bf", [P, DIM])
        wst = sb("wst", [P, HG, P])
        lam_sb = sb("lam_sb", [P, UNITS])
        gam_sb = sb("gam_sb", [P, UNITS])
        domcol = sb("domcol", [P, NDOM * EXP])
        idf = sb("idf", [P, P])
        idb = sb("idb", [P, P], BF16)
        rows32 = sb("rows32", [PARTS * 32, P])
        rows = sb("rows", [PARTS * 32, P], BF16)
        bo_part = sb("bo_part", [P, PARTS - 1, DIM], BF16)
        bo_rows = sb("bo_rows", [PARTS * 32, DIM], BF16)
        neg_idb = sb("neg_idb", [P, P], BF16)
        selv32 = sb("selv32", [P, NB, P])
        selv = sb("selv", [P, NB, P], BF16)
        sely = sb("sely", [P, NB, 32])
        rnd = sb("rnd", [P, 1])
        rnd_neg = sb("rnd_neg", [P, 1])
        one_root = sb("one_root", [P, 1])
        dom_i = sb("dom_i", [P, NTILE], I32)
        dom_f = sb("dom_f", [P, NTILE])
        tok = sb("tok", [P, NTILE, DIM])
        emb_t = sb("emb_t", [P, KD, T])
        act_t = sb("act_t", [P, KD, T])
        masked = sb("masked", [P, TT, DIM])
        tmp_f = sb("tmp_f", [P, TT, DIM])
        tmp_b = sb("tmp_b", [P, TT, DIM])
        xq = sb("xq", [P, TT, DIM], BF16)
        xq_t = sb("xq_t", [P, KD, T], BF16)
        kk = sb("kk", [P, 2, HG, T])
        q_sb = sb("q_sb", [P, HG, T])
        v_part = [sb(f"v_part{p}", [P, HG, T], BF16) for p in range(PARTS)]
        v_rows = sb("v_rows", [PARTS * 32, 2, HG, NA, T], BF16)
        y_t = sb("y_t", [P, HG, T])
        vg = sb("vg", [P, NVG, T])
        uu = sb("uu", [P, NU, T])
        carry = sb("carry", [P, UNITS])
        zz = sb("zz", [P, NZ, T])
        bn = sb("bn", [P, 2, TT, 6])
        mv = sb("mv", [P, 2, TT, 2])
        ve = sb("ve", [P, 2, TT])
        sd = sb("sd", [P, 2, TT])
        nr = sb("nr", [P, 2, 3, TT])
        rstd = sb("rstd", [P, 2, TT])
        nmr = sb("nmr", [P, 2, TT])
        am = sb("am", [P, TT])
        xs = sb("xs", [P, TT])
        xinv = sb("xinv", [P, TT])
        wam = sb("wam", [P, KD])
        ws = sb("ws", [P, KD])
        winv = sb("winv", [P, KD])

        vr_ps = ps("vr_ps", [P, NVR, T])
        q_ps = ps("q_ps", [P, HG, T])
        y_ps = ps("y_ps", [P, T])
        scr = ps("scr", [P, 2, T])
        r_ps = ps("r_ps", [P, T])
        scr_two = [scr[:, i, :].rearrange("p (b d) -> p b d", b=2) for i in range(2)]
        scr_bf = [scr[:, i, 0:T // 2].bitcast(BF16).rearrange("p (k t) -> p k t", k=KD) for i in range(2)]

        s_ids = sem("s_ids")
        s_ident, s_lam = sem("s_ident"), sem("s_lam")
        s_w_exp, s_w_proj, s_w_qkv, s_w_unit, s_w_back = (
            sem(n) for n in ("s_w_exp", "s_w_proj", "s_w_qkv", "s_w_unit", "s_w_back"))
        s_base = [[sem(f"s_base{c}_{h}") for h in range(2)] for c in range(NC)]
        s_dom = [[sem(f"s_dom{c}_{h}") for h in range(2)] for c in range(NC)]
        s_const = sem("s_const")
        s_scaled = sem("s_scaled")
        s_bk4 = sem("s_bk4")
        s_cast = sem("s_cast")
        s_sel = sem("s_sel")
        s_sig = sem("s_sig")
        s_ret = sem("s_ret")
        s_full = [sem("s_full0"), sem("s_full1")]
        s_free = [sem("s_free0"), sem("s_free1")]
        s_var = [sem("s_var1"), sem("s_var2")]
        s_sqrt = [sem("s_sqrt1"), sem("s_sqrt2")]
        s_rstd = [sem("s_rstd1"), sem("s_rstd2")]
        s_xhat = [sem("s_xhat1"), sem("s_xhat2")]
        s_vleft = [sem("s_vleft0"), sem("s_vleft1")]
        s_vpart = [sem("s_vhi"), sem("s_vmid")]
        s_vrows = [[sem(f"s_vrows{p}_{hg}") for hg in range(HG)] for p in range(PARTS)]
        s_amax = sem("s_amax")
        s_round = sem("s_round")
        s_xq = sem("s_xq")
        s_h2b = sem("s_h2b")
        s_out = sem("s_out")
        s_domf = sem("s_domf")
        s_stored = sem("s_stored")
        s_vr = sem("s_vr")
        s_vg = sem("s_vg")
        s_u = sem("s_u")
        s_scan = sem("s_scan")
        s_carry = sem("s_carry")
        s_z = sem("s_z")
        s_y = sem("s_y")
        s_yt = sem("s_yt")
        s_bo = sem("s_bo")
        s_wq = sem("s_wq")
        s_dve = sem("s_dve")

        def moves(c, hg):
            return c + 1 if hg else c

        def filled(eng, name, c, h):
            bank, before = use[name, c, h]
            eng.wait_ge(s_full[bank], before + 1)
            return bank

        def taken(eng, name, c, h):
            bank, before = use[name, c, h]
            eng.wait_ge(s_free[bank], before + 1)

        block = ctx.enter_context(nc.Block())

        @block.sync
        def _(sp):
            sp.dma_start(ids_sb[:], ids).then_inc(s_ids, 16)
            sp.dma_start(idf[:], ident).then_inc(s_ident, 16)
            sp.dma_start(lam_sb[:], lam).then_inc(s_lam, 16)
            for dst, src in ((wexp, w_exp), (domcol, dom_of_col)):
                sp.dma_start(dst[:], src).then_inc(s_w_exp, 16)
            sp.dma_start(wproj[:], w_proj).then_inc(s_w_proj, 16)
            for dst, src in ((wv, w_v), (bv, b_v), (wk, w_k), (bk, b_k), (wq, w_q), (bq, b_q)):
                sp.dma_start(dst[:], src).then_inc(s_w_qkv, 16)
            for dst, src in ((gam_sb, gam), (wst, static), (selv32, sel_v), (sely, sel_y)):
                sp.dma_start(dst[:], src).then_inc(s_w_unit, 16)
            for dst, src in ((wf, w_f), (wo, w_o), (bo, b_o), (rows32, first_rows), (bf, b_f)):
                sp.dma_start(dst[:], src).then_inc(s_w_back, 16)
            out_v = out.rearrange("b (c t p) d -> (b c) p t d", c=2 * SEQ // T, p=P)

            def move_v(c):
                if c >= 2:
                    sp.wait_ge(s_vr, UNITS * (c - 1))
                for hg in range(HG):
                    if c == 0 and hg == 0:
                        continue
                    for p in range(PARTS):
                        if p < PARTS - 1:
                            sp.wait_ge(s_vpart[p], HG * c + hg + 1)
                        else:
                            taken(sp, "v", c, hg)
                        for a in range(NA):
                            sp.dma_start(v_rows[32 * p:32 * p + 32, c % 2, hg, a, :],
                                         v_part[p][32 * a:32 * a + 32, hg, :]).then_inc(s_vrows[p][hg], 16)

            def store(c):
                for h in range(2):
                    if c < NC - 1:
                        sp.wait_ge(s_out, 2 * c + h + 1)
                    else:
                        taken(sp, "ffn", c, h)
                    sp.dma_start(out_v[2 * c + h], tok[:, TT * c + 2 * h:TT * c + 2 * h + 2, :])\
                      .then_inc(s_stored, 16)

            move_v(0)
            for c in range(1, NC):
                if c >= 2:
                    store(c - 2)
                move_v(c)
            store(NC - 2)
            store(NC - 1)
            sp.wait_ge(s_stored, 16 * 2 * NC)

        @block.gpsimd
        def _(pool):
            pool.wait_ge(s_ids, 16)

            def gather(c, t):
                ix = bass.IndirectOffsetOnAxis(ap=ids_sb[:, TT * c + t:TT * c + t + 1], axis=0)
                pool.indirect_dma_start(tok[:, TT * c + t, :], None, table, ix).then_inc(s_base[c][t // 2], 16)

            def domain(c, t):
                ix = bass.IndirectOffsetOnAxis(ap=ids_sb[:, TT * c + t:TT * c + t + 1], axis=0)
                pool.indirect_dma_start(dom_i[:, TT * c + t:TT * c + t + 1], None, domain_map, ix)\
                    .then_inc(s_dom[c][t // 2], 16)

            def bias(c, _):
                pool.wait_ge(s_xhat[1], 2 * c + 2)
                if c == 0:
                    pool.wait_ge(s_w_back, 80)
                h = tok[:, TT * c:TT * c + TT, :]
                pool.tensor_tensor(h, h, bf[:].rearrange("p (o d) -> p o d", o=1).to_broadcast([P, TT, DIM]),
                                   ALU.add).then_inc(s_h2b, 1)

            def out_(c, h):
                taken(pool, "ffn", c, h)
                pool.wait_ge(s_h2b, c + 1)
                x = tok[:, TT * c + 2 * h:TT * c + 2 * h + 2, :]
                pool.tensor_tensor(x, x, tmp_b[:, 2 * h:2 * h + 2, :], ALU.add).then_inc(s_out, 1)

            stage = {"bias": bias, "out": out_}
            for c in range(NC):
                for t in range(TT):
                    gather(c, t)
                for t in range(TT):
                    domain(c, t)
            for c in range(1, NC):
                for h in range(2):
                    pool.wait_ge(s_dom[c][h], 16 * 2)
            pool.tensor_copy(dom_f[:, TT:], dom_i[:, TT:]).then_inc(s_domf, 1)
            for slot in SLOTS:
                if 0 <= slot < NC * UNITS:
                    c, n, hg, a, b = unit(slot)
                    if n % HD == 0:
                        taken(pool, "k", c, hg)
                    pool.wait_ge(s_vg, slot + 1)
                    if slot >= NU:
                        pool.wait_ge(s_scan, slot - NU + 1)
                    pool.tensor_tensor(uu[:, slot % NU, :], vg[:, slot % NVG, :], kk[:, c % 2, hg, :],
                                       ALU.mult).then_inc(s_u, 1)
                for name, c, h in pool_at.get(slot, []):
                    stage[name](c, h)

        @block.scalar
        def _(act):
            act.wait_ge(s_lam, 16)
            act.activation(lam_sb[:], lam_sb[:], ACT.Sigmoid).then_inc(s_sig, 1)
            act.wait_ge(s_const, 1)
            act.activation(one_root[:], rnd[:], ACT.Sqrt)
            act.wait_ge(s_ident, 16)
            act.activation(idb[:], idf[:], ACT.Copy).then_inc(s_cast, 1)
            act.activation(neg_idb[:], idf[:], ACT.Copy, scale=-1.0).then_inc(s_cast, 1)

            def w_scale(*_):
                act.wait_ge(s_w_proj, 16)
                act.activation(wproj[:], wproj[:], ACT.Copy, scale=0.1).then_inc(s_scaled, 1)

            def b_scale(*_):
                act.wait_ge(s_w_qkv, 96)
                act.activation(bk4[:], bk[:], ACT.Copy, scale=HD ** -0.5).then_inc(s_bk4, 1)

            def select(*_):
                act.wait_ge(s_w_unit, 64)
                act.activation(selv[:], selv32[:], ACT.Copy).then_inc(s_sel, 1)

            def evacuate(name, dst, reader):
                def step(c, h):
                    bank = filled(act, name, c, h)
                    if c >= 1 and reader:
                        filled(act, reader[0], c - 1, h if reader[1] is None else reader[1])
                    act.activation(dst[:, :, T // 2 * h:T // 2 * (h + 1)], scr_two[bank], ACT.Copy)\
                       .then_inc(s_free[bank], 1)
                return step

            def residual(name):
                def step(c, h):
                    bank = filled(act, name, c, h)
                    act.activation(tok[:, TT * c + 2 * h:TT * c + 2 * h + 2, :], scr_two[bank], ACT.Copy)\
                       .then_inc(s_free[bank], 1)
                return step

            def q(c, hg):
                bank = filled(act, "q", c, hg)
                if c >= 1:
                    act.wait_ge(s_y, (UNITS * (c - 1) + HD * (hg + 1)) // NA)
                act.activation(q_sb[:, hg, :], scr[:, bank, :], ACT.Identity, bias=bq[:, hg:hg + 1])
                act.activation(q_ps[:, hg, :], scr[:, bank, :], ACT.Identity, bias=bq[:, hg:hg + 1])\
                   .then_inc(s_free[bank], 1)

            def v_part_of(p):
                def step(c, hg):
                    bank = filled(act, "v", c, hg)
                    if p:
                        act.wait_ge(s_vleft[p - 1], HG * c + hg + 1)
                    if c >= 1 and moves(c - 1, hg):
                        act.wait_ge(s_vrows[p][hg], 16 * NA * moves(c - 1, hg))
                    if c >= 1 and hg == 0:
                        act.wait_ge(s_vr, UNITS * (c - 1) + (DIRECT if c > 1 else HD))
                    act.activation(v_part[p][:, hg, :], scr[:, bank, :], ACT.Identity, bias=bv[:, hg:hg + 1])\
                       .then_inc(s_free[bank] if p == PARTS - 1 else s_vpart[p], 1)
                return step

            def k(c, hg):
                bank = filled(act, "k", c, hg)
                if c == 0:
                    act.wait_ge(s_bk4, 1)
                if c >= 2:
                    act.wait_ge(s_u, UNITS * (c - 1))
                act.activation(kk[:, c % 2, hg, :], scr[:, bank, :], ACT.Identity, bias=bk4[:, hg:hg + 1],
                               scale=HD ** -0.5).then_inc(s_free[bank], 1)

            def y(c, hg):
                act.wait_ge(s_y, (UNITS * c + HD * (hg + 1)) // NA)
                if c >= 1:
                    filled(act, "attn", c - 1, 1)
                act.activation(y_t[:, hg, :], y_ps[:], ACT.Copy).then_inc(s_yt, 1)

            def sqrt(n):
                def step(c, h):
                    act.wait_ge(s_var[n], 2 * c + h + 1)
                    two = slice(2 * h, 2 * h + 2)
                    act.activation(sd[:, n, two], ve[:, n, two], ACT.Sqrt).then_inc(s_sqrt[n], 1)
                return step

            def xhat(n, dst):
                def step(c, h):
                    if n == 0 and c >= 1:
                        filled(act, "xhat_t", c - 1, h)
                    if n == 1 and c >= 1:
                        act.wait_ge(s_out, 2 * c + h - 1)
                    act.wait_ge(s_rstd[n], 2 * c + h + 1)
                    for t in (2 * h, 2 * h + 1):
                        last = act.activation(dst[:, t, :], tok[:, TT * c + t, :], ACT.Identity,
                                              bias=nmr[:, n, t:t + 1], scale=rstd[:, n, t:t + 1])
                    last.then_inc(s_xhat[n], 1)
                return step

            def quant(c, h):
                act.wait_ge(s_amax, 2 * c + h + 1)
                for t in (2 * h, 2 * h + 1):
                    last = act.activation(tmp_b[:, t, :], tmp_b[:, t, :], ACT.Identity, bias=rnd[:],
                                          scale=xinv[:, t:t + 1])
                last.then_inc(s_round, 1)
                act.wait_ge(s_round, 2 * c + h + 1)
                if c >= 1:
                    filled(act, "xq_t", c - 1, h)
                two = slice(2 * h, 2 * h + 2)
                act.activation(xq[:, two, :], tmp_b[:, two, :], ACT.Identity, bias=rnd_neg[:]).then_inc(s_xq, 1)

            def scaled(c, h):
                bank = filled(act, "ffn", c, h)
                act.wait_ge(s_amax, 2 * c + h + 1)
                for i in range(2):
                    t = 2 * h + i
                    last = act.activation(tmp_b[:, t, :], scr_two[bank][:, i, :], ACT.Copy, scale=xs[:, t:t + 1])
                last.then_inc(s_free[bank], 1)

            def xq_evac(c, h):
                bank = filled(act, "xq_t", c, h)
                if c >= 1:
                    filled(act, "ffn", c - 1, h)
                act.activation(xq_t[:, :, T // 2 * h:T // 2 * (h + 1)], scr_bf[bank], ACT.Copy)\
                   .then_inc(s_free[bank], 1)

            def bo_hi(*_):
                act.wait_ge(s_w_back, 80)
                act.activation(rows[:], rows32[:], ACT.Copy)
                act.activation(bo_part[:, 0, :], bo[:], ACT.Copy).then_inc(s_bo, 1)

            def bo_mid(*_):
                act.wait_ge(s_bo, 2)
                act.activation(bo_rows[0:32, :], bo_part[0:32, 0, :], ACT.Copy)
                act.activation(bo_rows[32:64, :], bo[32:64, :], ACT.Copy)
                act.activation(bo_part[:, 1, :], bo[:], ACT.Copy).then_inc(s_bo, 1)

            def bo_lo(*_):
                act.wait_ge(s_bo, 4)
                act.activation(bo_rows[64:96, :], bo[64:96, :], ACT.Copy).then_inc(s_bo, 1)

            def w_round(*_):
                act.wait_ge(s_wq, 1)
                for k_ in range(KD):
                    last = act.activation(wf[:, k_, :], wf[:, k_, :], ACT.Identity, bias=rnd[:],
                                          scale=winv[:, k_:k_ + 1])
                last.then_inc(s_wq, 1)

            def w_hi(*_):
                for k_ in range(KD):
                    bank = filled(act, "w_t", 0, k_)
                    last = act.activation(wf_parts[:, 0, k_, :], scr[:, bank, 0:DIM], ACT.Copy)
                last.then_inc(s_wq, 1)

            def w_mid(*_):
                taken(act, "w_t", 0, 0)
                taken(act, "w_t", 0, 1)
                act.activation(wf_parts[:, 1], wf[:], ACT.Copy).then_inc(s_wq, 1)

            stage = {"base_t": evacuate("base_t", emb_t, ("corr", None)),
                     "masked_t": evacuate("masked_t", emb_t, None),
                     "xhat_t": evacuate("xhat_t", act_t, ("q", 1)), "corr": residual("corr"),
                     "attn": residual("attn"), "q": q, "v_hi": v_part_of(0), "v_mid": v_part_of(1),
                     "v_lo": v_part_of(2), "k": k, "y": y, "sqrt1": sqrt(0), "sqrt2": sqrt(1),
                     "xhat": xhat(0, tmp_f), "xhat2": xhat(1, tmp_b), "quant": quant, "xq_t": xq_evac,
                     "scaled": scaled, "w_scale": w_scale, "b_scale": b_scale, "select": select,
                     "w_round": w_round, "bo_hi": bo_hi, "bo_mid": bo_mid, "bo_lo": bo_lo, "w_hi": w_hi,
                     "w_mid": w_mid}
            for slot in SLOTS:
                if 0 <= slot < NC * UNITS:
                    act.wait_ge(s_vr, slot + 1)
                    if slot >= NVG:
                        act.wait_ge(s_u, slot - NVG + 1)
                    n = slot % UNITS
                    act.activation(vg[:, slot % NVG, :], vr_ps[:, slot % NVR, :], ACT.Copy,
                                   scale=gam_sb[:, n:n + 1]).then_inc(s_vg, 1)
                for name, c, h in act_at.get(slot, []):
                    stage[name](c, h)

        @block.vector
        def _(dve):
            chain = [0]
            saved = {}

            def link(ins):
                chain[0] += 1
                ins.then_inc(s_dve, 1)
                dve.wait_ge(s_dve, chain[0])

            dve.memset(rnd[:], ROUND)
            dve.memset(rnd_neg[:], -ROUND).then_inc(s_const, 1)
            dve.wait_ge(s_sig, 1)
            dve.tensor_scalar(r_ps[:, 0:UNITS], lam_sb[:], -1.0, 1.0, ALU.mult, ALU.add).then_inc(s_ret, 1)
            dve.wait_ge(s_w_exp, 32)

            def mask(c, h):
                if c == 0:
                    dve.wait_ge(s_dom[0][h], 16 * 2)
                    two = slice(2 * h, 2 * h + 2)
                    link(dve.tensor_copy(dom_f[:, two], dom_i[:, two]))
                else:
                    dve.wait_ge(s_domf, 1)
                bank = filled(dve, "expand", c, h)
                if c >= 1:
                    filled(dve, "masked_t", c - 1, h)
                for i in range(2):
                    t = 2 * h + i
                    last = dve.scalar_tensor_tensor(masked[:, t, :], domcol[:], dom_f[:, TT * c + t:TT * c + t + 1],
                                                    scr_two[bank][:, i, :], ALU.is_equal, ALU.mult)
                last.then_inc(s_free[bank], 1)

            def stats(n, name):
                def step(c, h):
                    taken(dve, name, c, h)
                    for t in (2 * h, 2 * h + 1):
                        last = dve.bn_stats(bn[:, n, t, :], tok[:, TT * c + t, :])
                    link(last)
                    for t in (2 * h, 2 * h + 1):
                        last = dve.bn_aggr(mv[:, n, t, :], bn[:, n, t, :])
                    link(last)
                    two = slice(2 * h, 2 * h + 2)
                    dve.tensor_scalar(ve[:, n, two], mv[:, n, two, 1], LNEPS, None, ALU.add).then_inc(s_var[n], 1)
                return step

            def rsqrt(n):
                def step(c, h):
                    dve.wait_ge(s_sqrt[n], 2 * c + h + 1)
                    two = slice(2 * h, 2 * h + 2)
                    r0, half_sq, fix = (nr[:, n, i, two] for i in range(3))
                    link(dve.reciprocal(r0, sd[:, n, two]))
                    link(dve.scalar_tensor_tensor(half_sq, r0, -0.5, r0, ALU.mult, ALU.mult))
                    link(dve.tensor_tensor(fix, half_sq, ve[:, n, two], ALU.mult))
                    link(dve.scalar_tensor_tensor(rstd[:, n, two], fix, 1.5, r0, ALU.add, ALU.mult))
                    dve.scalar_tensor_tensor(nmr[:, n, two], mv[:, n, two, 0], -1.0, rstd[:, n, two], ALU.mult,
                                             ALU.mult).then_inc(s_rstd[n], 1)
                return step

            def amax(c, h):
                dve.wait_ge(s_xhat[1], 2 * c + h + 1)
                if c >= 1:
                    taken(dve, "ffn", c - 1, h)
                two = slice(2 * h, 2 * h + 2)
                link(dve.tensor_reduce(am[:, two], tmp_b[:, two, :], AX.X, ALU.max, apply_absolute_value=True))
                link(dve.tensor_scalar(xs[:, two], am[:, two], QEPS, 1.0 / QMAX, ALU.max, ALU.mult))
                dve.reciprocal(xinv[:, two], xs[:, two]).then_inc(s_amax, 1)

            def finish(c, h):
                bank = filled(dve, "ffn", c, h)
                if h == 0:
                    dve.wait_ge(s_h2b, c + 1)
                for i in range(2):
                    t = 2 * h + i
                    x = tok[:, TT * c + t, :]
                    last = dve.scalar_tensor_tensor(x, scr_two[bank][:, i, :], xs[:, t:t + 1], x, ALU.mult, ALU.add)
                last.then_inc(s_free[bank], 1)

            def bo_less(*_):
                dve.wait_ge(s_bo, 1)
                dve.tensor_tensor(bo[:], bo[:], bo_part[:, 0, :], ALU.subtract).then_inc(s_bo, 1)

            def bo_less2(*_):
                dve.wait_ge(s_bo, 3)
                dve.tensor_tensor(bo[:], bo[:], bo_part[:, 1, :], ALU.subtract).then_inc(s_bo, 1)

            def w_amax(*_):
                dve.wait_ge(s_w_back, 80)
                link(dve.tensor_reduce(wam[:], wf[:], AX.X, ALU.max, apply_absolute_value=True))
                link(dve.tensor_scalar(ws[:], wam[:], QEPS, 1.0 / QMAX, ALU.max, ALU.mult))
                dve.reciprocal(winv[:], ws[:]).then_inc(s_wq, 1)

            def w_deq(*_):
                dve.wait_ge(s_wq, 2)
                for k_ in range(KD):
                    last = dve.tensor_scalar(wf[:, k_, :], wf[:, k_, :], -ROUND, ws[:, k_:k_ + 1], ALU.add, ALU.mult)
                last.then_inc(s_wq, 1)

            def w_res(*_):
                dve.wait_ge(s_wq, 4)
                for k_ in range(KD):
                    bank = filled(dve, "w_t", 0, k_)
                    dve.tensor_tensor(wf[:, k_, :], scr[:, bank, 0:DIM], wf_parts[:, 0, k_, :], ALU.subtract)\
                       .then_inc(s_free[bank], 1)

            def w_lo(*_):
                dve.wait_ge(s_wq, 5)
                dve.tensor_tensor(wf_parts[:, 2], wf[:], wf_parts[:, 1], ALU.subtract).then_inc(s_wq, 1)

            def scan(g):
                c, n, hg, a, b = unit(g)
                dve.wait_ge(s_u, g + 1)
                if g >= NZ:
                    dve.wait_ge(s_y, (g - NZ) // NA + 1)
                start = 0.0 if c % (SEQ // T) == 0 else carry[:, n:n + 1]
                dve.tensor_tensor_scan(zz[:, g % NZ, :], r_ps[:, n:n + 1].to_broadcast([P, T]), uu[:, g % NU, :],
                                       start, ALU.mult, ALU.add).then_inc(s_scan, 1)

            def keep(g):
                c, n, hg, a, b = unit(g)
                if (c + 1) % (SEQ // T):
                    saved[g] = len(saved) + 1
                    dve.wait_ge(s_scan, g + 2)
                    dve.tensor_copy(carry[:, n:n + 2], zz[:, g % NZ:g % NZ + 2, T - 1]).then_inc(s_carry, 1)

            def product(g):
                c, n, hg, a, b = unit(g)
                if n % HD == 0:
                    taken(dve, "q", c, hg)
                dve.wait_ge(s_scan, g + 2)
                x = zz[:, g % NZ:g % NZ + 2, :]
                if (c + 1) % (SEQ // T):
                    dve.wait_ge(s_carry, saved[g])
                q = q_ps[:, hg, :].rearrange("p (o t) -> p o t", o=1).to_broadcast([P, 2, T])
                dve.tensor_tensor(x, x, q, ALU.mult).then_inc(s_z, 1)

            stage = {"mask": mask, "stat1": stats(0, "corr"), "rstd1": rsqrt(0), "stat2": stats(1, "attn"),
                     "rstd2": rsqrt(1), "amax": amax, "out": finish, "w_amax": w_amax, "bo_less": bo_less,
                     "bo_less2": bo_less2, "w_deq": w_deq, "w_res": w_res, "w_lo": w_lo}
            for slot in SLOTS:
                if 2 < slot <= NC * UNITS + 1 and slot % 2:
                    keep(slot - 3)
                if 0 <= slot < NC * UNITS:
                    if slot == 0:
                        dve.wait_ge(s_ret, 1)
                    scan(slot)
                if 2 < slot <= NC * UNITS + 1 and slot % 2:
                    product(slot - 3)
                for name, c, h in dve_at.get(slot, []):
                    stage[name](c, h)

        @block.tensor
        def _(pe):
            def scratch(name, c, h):
                bank, before = use[name, c, h]
                if before:
                    pe.wait_ge(s_free[bank], before)
                return bank

            def transposes(name, src, wait, ident_, view):
                def step(c, h):
                    bank = scratch(name, c, h)
                    wait(c, h)
                    for i in range(2):
                        for k_ in range(KD):
                            last = pe.transpose(view[bank][:, k_, P * i:P * i + P],
                                                src(c, 2 * h + i)[:, P * k_:P * k_ + P], ident_[:])
                    last.then_inc(s_full[bank], 1)
                return step

            def token_major(name, weight):
                def step(c, h):
                    bank = scratch(name, c, h)
                    if c == 0:
                        pe.wait_ge(s_w_exp, 32)
                        if name == "corr":
                            pe.wait_ge(s_scaled, 1)
                    for i in range(2):
                        t = 2 * h + i
                        for k_ in range(KD):
                            last = pe.matmul(scr_two[bank][:, i, :], emb_t[:, k_, P * t:P * t + P], weight[:, k_, :],
                                             start=(k_ == 0), stop=(k_ == KD - 1 and name == "expand"))
                        if name == "corr":
                            last = pe.matmul(scr_two[bank][:, i, :], idf[:], tok[:, TT * c + t, :],
                                             start=False, stop=True)
                    last.then_inc(s_full[bank], 1)
                return step

            def channel_major(name, weight):
                def step(c, hg):
                    bank = scratch(name, c, hg)
                    if c == 0:
                        pe.wait_ge(s_w_qkv, 96)
                    for k_ in range(KD):
                        last = pe.matmul(scr[:, bank, :], weight[:, k_, P * hg:P * hg + P], act_t[:, k_, :],
                                         start=(k_ == 0), stop=(k_ == KD - 1))
                    last.then_inc(s_full[bank], 1)
                return step

            def v(c, hg):
                bank = scratch("v", c, hg)
                if c == 0:
                    pe.wait_ge(s_w_qkv, 96)
                for k_ in range(KD):
                    last = pe.matmul(scr[:, bank, :], wv[:, k_, P * hg:P * hg + P], act_t[:, k_, :],
                                     start=(k_ == 0), stop=(k_ == KD - 1))
                last.then_inc(s_full[bank], 1)

            def v_less(p):
                def step(c, hg):
                    bank, _ = use["v", c, hg]
                    pe.wait_ge(s_vpart[p], HG * c + hg + 1)
                    if c == 0:
                        pe.wait_ge(s_cast, 2)
                    pe.matmul(scr[:, bank, :], neg_idb[:], v_part[p][:, hg, :], start=False, stop=True,
                              skip_group_check=True).then_inc(s_vleft[p], 1)
                return step

            def attn(c, h):
                bank = scratch("attn", c, h)
                pe.wait_ge(s_yt, HG * (c + 1))
                if c == 0:
                    pe.wait_ge(s_w_back, 80)
                    pe.wait_ge(s_bo, 5)
                for i in range(2):
                    t = 2 * h + i
                    x = scr_two[bank][:, i, :]
                    pe.matmul(x, rows[:], bo_rows[:], start=True, stop=False)
                    pe.matmul(x, idf[:], tok[:, TT * c + t, :], start=False, stop=False)
                    for hg in range(HG):
                        last = pe.matmul(x, y_t[:, hg, P * t:P * t + P], wo[:, hg, :],
                                         start=False, stop=(hg == HG - 1))
                last.then_inc(s_full[bank], 1)

            def ffn(c, h):
                bank = scratch("ffn", c, h)
                if c == 0:
                    pe.wait_ge(s_wq, 6)
                taken(pe, "xq_t", c, h)
                for i in range(2):
                    t = 2 * h + i
                    for n in range(PARTS * KD):
                        p, k_ = n // KD, n % KD
                        last = pe.matmul(scr_two[bank][:, i, :], xq_t[:, k_, P * t:P * t + P], wf_parts[:, p, k_, :],
                                         start=(n == 0), stop=(n == PARTS * KD - 1))
                last.then_inc(s_full[bank], 1)

            def wake(c, n):
                if c == 0:
                    bank = y_ps[:]
                else:
                    bank = vr_ps[:, 0, :]
                    pe.wait_ge(s_vg, NC * UNITS)
                for _ in range(n):
                    pe.matmul(bank[:, 0:P], idf[:], idf[:], start=True, stop=True)

            def w_t(_, k_):
                bank = scratch("w_t", 0, k_)
                pe.wait_ge(s_wq, 3)
                for o in range(KD):
                    last = pe.transpose(scr[:, bank, P * o:P * o + P], wf[:, o, P * k_:P * k_ + P], idf[:])
                last.then_inc(s_full[bank], 1)

            stage = {"base_t": transposes("base_t", lambda c, t: tok[:, TT * c + t, :],
                                     lambda c, h: pe.wait_ge(s_base[c][h], 16 * 2), idf, scr_two),
                     "expand": token_major("expand", wexp),
                     "masked_t": transposes("masked_t", lambda c, t: masked[:, t, :],
                                     lambda c, h: taken(pe, "expand", c, h), idf, scr_two),
                     "corr": token_major("corr", wproj),
                     "xhat_t": transposes("xhat_t", lambda c, t: tmp_f[:, t, :],
                                     lambda c, h: pe.wait_ge(s_xhat[0], 2 * c + h + 1), idf, scr_two), "v": v,
                     "v_less": v_less(0), "v_less2": v_less(1), "k": channel_major("k", wk),
                     "q": channel_major("q", wq), "xq_t": transposes("xq_t", lambda c, t: xq[:, t, :],
                                     lambda c, h: pe.wait_ge(s_xq, 2 * c + h + 1), idb, scr_bf), "attn": attn,
                     "ffn": ffn, "w_t": w_t, "wake": wake}
            operand = {"expand": "base_t", "corr": "masked_t", "v": "xhat_t", "k": "xhat_t", "q": "xhat_t"}

            def spread(g):
                c, n, hg, a, b = unit(g)
                direct = DIRECT if c else HD
                if n == HD or n == direct:
                    for p in range(PARTS):
                        pe.wait_ge(s_vrows[p][hg], 16 * NA * moves(c, hg))
                if g >= NVR:
                    pe.wait_ge(s_vg, g - NVR + 1)
                if n < direct:
                    if n == 0:
                        taken(pe, "v", c, 0)
                    rows_a = slice(32 * a, 32 * a + 32)
                    for p in range(PARTS):
                        last = pe.matmul(vr_ps[:, g % NVR, :], selv[rows_a, b, :], v_part[p][rows_a, 0, :],
                                         start=(p == 0), stop=(p == PARTS - 1))
                    last.then_inc(s_vr, 1)
                    return
                pe.matmul(vr_ps[:, g % NVR, :], selv[0:PARTS * 32, b, :], v_rows[:, c % 2, hg, a, :],
                          start=True, stop=True).then_inc(s_vr, 1)

            def collect(g):
                c, n, hg, a, b = unit(g)
                if n % HD == 0 and g > 0:
                    pe.wait_ge(s_yt, g // HD)
                if b == 0:
                    taken(pe, "q", c, hg)
                    pe.matmul(y_ps[:], wst[:, hg, :], q_sb[:, hg, :], start=True, stop=True)
                pe.wait_ge(s_z, (g + NA) // 2)
                for a in range(NA):
                    last = pe.matmul(y_ps[32 * a:32 * a + 32, :], sely[:, b, :], zz[:, (g + a) % NZ, :],
                                     start=False, stop=True, skip_group_check=True)
                last.then_inc(s_y, 1)

            pe.wait_ge(s_ident, 16)
            wake(0, WAKE)
            for slot in SLOTS:
                if slot == 0:
                    pe.wait_ge(s_sel, 1)
                if 0 <= slot < NC * UNITS:
                    spread(slot)
                g = slot - LAG - NA + 1
                if g >= 0 and g % NA == 0 and g < NC * UNITS:
                    collect(g)
                for name, c, h in pe_at.get(slot, []):
                    if name in ("v", "k", "q"):
                        taken(pe, operand[name], c, 0)
                        taken(pe, operand[name], c, 1)
                    elif name in operand:
                        taken(pe, operand[name], c, h)
                    stage[name](c, h)


def kernel(**inputs):
    import concourse.bacc as _bacc
    from concourse.bass_utils import run_bass_kernel_spmd as _run

    def halves(m):
        return m.reshape(KD, P, -1).transpose(1, 0, 2)

    g = {k: np.asarray(v) for k, v in inputs.items()}
    rows = np.arange(DIM).reshape(HG, P // HD, NA, NB).transpose(0, 2, 1, 3).reshape(-1)
    w_qkv, b_qkv = g["L0_attn_Wqkv_w"], g["L0_attn_Wqkv_b"]

    def per_unit(m):
        m = m.reshape(HG, P // HD, NA, NB, HD).transpose(1, 4, 0, 3, 2)
        return m.reshape(P, UNITS)

    h8 = np.arange(P) // HD
    sel_v = np.zeros((NA, P // HD, NB, NB, P), np.float32)
    sel_y = np.zeros((P, NB, P // HD, NB), np.float32)
    for b in range(NB):
        for h in range(P // HD):
            sel_v[:, h, b, b, h8 == h] = 1.0
            sel_y[h8 == h, b, h, b] = 1.0
    first_rows = np.zeros((PARTS * 32, P), np.float32)
    first_rows[::32] = 1.0
    static = np.zeros((P // HD, HD, HG, NA, P // HD, NB), np.float32)
    w = g["L0_attn_W_static"].reshape(HG, P // HD, NA, NB, HD)
    for h in range(P // HD):
        static[h, :, :, :, h, :] = w[:, h].transpose(3, 0, 1, 2)
    static = static.reshape(P, HG, P)
    arrays = {
        "ids": g["x"].reshape(NTILE, P).T,
        "domain_map": g["L0_tok_domain_map"].reshape(-1, 1),
        "table": g["L0_tok_emb_table"],
        "w_exp": halves(g["L0_tok_W_exp"].reshape(NDOM * EXP, DIM).T),
        "w_proj": halves(g["L0_tok_W_proj"].transpose(0, 2, 1).reshape(NDOM * EXP, DIM)),
        "w_q": halves(w_qkv[:DIM].T),
        "w_k": halves(w_qkv[DIM:2 * DIM].T),
        "w_v": halves(w_qkv[2 * DIM:][rows].T),
        "b_q": b_qkv[:DIM].reshape(HG, P).T,
        "b_k": b_qkv[DIM:2 * DIM].reshape(HG, P).T,
        "b_v": b_qkv[2 * DIM:][rows].reshape(HG, P).T,
        "w_o": halves(g["L0_attn_out_w"].T[rows]),
        "b_o": np.broadcast_to(g["L0_attn_out_b"], (P, DIM)),
        "static": static,
        "lam": per_unit(g["L0_attn_Lambda_raw"]),
        "gam": per_unit(g["L0_attn_Gamma"]),
        "w_f": halves(g["L0_ffn_weight"]),
        "b_f": np.broadcast_to(g["L0_ffn_bias"], (P, DIM)),
        "dom_of_col": np.broadcast_to(np.arange(NDOM * EXP, dtype=np.float32) // EXP, (P, NDOM * EXP)),
        "ident": np.eye(P, dtype=np.float32),
        "first_rows": first_rows,
        "sel_v": sel_v.reshape(P, NB, P),
        "sel_y": sel_y.reshape(P, NB, 32),
    }
    nc = _bacc.Bacc("TRN2", target_bir_lowering=False, num_devices=1)
    args = {}
    for name, a in arrays.items():
        arrays[name] = a = np.ascontiguousarray(a)
        args[name] = nc.dram_tensor(f"in_{name}", a.shape, mybir.dt.from_np(a.dtype), kind="ExternalInput").ap()
    out = nc.dram_tensor("out_h", (BATCH, SEQ, DIM), F32, kind="ExternalOutput").ap()
    tower_kernel(nc, out=out, **args)
    r = _run(nc, [{f"in_{name}": a for name, a in arrays.items()}], core_ids=[0])
    return r.results[0]["out_h"]
```
